# Optimizing a Trainium2 kernel written in Bass

```python
import numpy as np
import jax
import jax.numpy as jnp

def _softmax(x, axis=-1):
    return jax.nn.softmax(x, axis=axis)

def _gelu(x):
    return jax.nn.gelu(x, approximate=True)

def _silu(x):
    return jax.nn.silu(x)

def _sigmoid(x):
    return jax.nn.sigmoid(x)

def _layernorm(x, axis=-1, eps=1e-05):
    m = jnp.mean(x, axis=axis, keepdims=True)
    v = jnp.var(x, axis=axis, keepdims=True)
    return (x - m) / jnp.sqrt(v + eps)

def _scatter_add(tgt, idx, src, axis=0):
    return tgt.at[idx].add(src)

def _segment_sum(src, seg, n):
    return jax.ops.segment_sum(src, seg, n)
kernel_name = 'mk_adj_resnorm_d4_adj_r2_b1f5b5'

def setup_inputs(seed: int=0):
    np.random.seed(seed)
    _w = jnp.asarray

    def _rec_inputs():
        import jax
        import jax.numpy as jnp
        _gk = jax.random.key(seed)
        x = -0.0002928 + 1 * jax.random.normal(jax.random.fold_in(_gk, 1), (128, 128, 128), jnp.float32)
        _a = jax.random.bernoulli(jax.random.fold_in(_gk, 2), 0.125, (128, 128, 128))
        _a = jnp.logical_or(_a, jnp.eye(128, dtype=bool))
        _af = _a.astype(jnp.float32)
        _af = _af * jax.random.uniform(jax.random.fold_in(_gk, 3), (128, 128, 128), jnp.float32, 0.05, 1)
        adj = _af
        _nm = jnp.ones((128, 128), dtype=bool)
        nodemask = jnp.where(_nm, 1.0, 0.0).astype(jnp.float32)
        return (x, adj, nodemask)
    x, adj, nodemask = _rec_inputs()

    def _L0_gnn_setup():
        import jax, jax.numpy as jnp
        import numpy as np
        D_IN = 128
        D_OUT = 128
        key = jax.random.key(seed)
        k1, k2, k3 = jax.random.split(key, 3)
        B, N = (4, 2048)
        seq = jax.random.normal(k1, (B, N, D_IN), dtype=jnp.float32)
        adj = jax.random.uniform(k2, (B, N, N), dtype=jnp.float32)
        limit = float(np.sqrt(6.0 / (D_IN + D_OUT)))
        W = jax.random.uniform(k3, (D_IN, D_OUT), dtype=jnp.float32, minval=-limit, maxval=limit)
        bias = jnp.zeros((D_OUT,), dtype=jnp.float32)
        prelu_a = jnp.array(0.25, dtype=jnp.float32)
        return {'seq': seq, 'adj': adj, 'W': W, 'bias': bias, 'prelu_a': prelu_a}
    _L0_gnn_all = _L0_gnn_setup()
    _L0_gnn_in = {k: v for k, v in _L0_gnn_all.items() if k in ('W', 'bias', 'prelu_a')}
    del _L0_gnn_all

    def _L1_gnn_setup():
        import jax, jax.numpy as jnp
        import numpy as np
        key = jax.random.key(seed)
        k1, k2, k3, k4 = jax.random.split(key, 4)
        B, N, F_in, F_out = (8, 1024, 128, 128)
        x = jax.random.normal(k1, (B, N, F_in), dtype=jnp.float32)
        adj = jax.random.uniform(k2, (B, N, N), dtype=jnp.float32)
        stdv = 1.0 / np.sqrt(F_out)
        weight = jax.random.uniform(k3, (F_in, F_out), dtype=jnp.float32, minval=-stdv, maxval=stdv)
        bias = jax.random.uniform(k4, (F_out,), dtype=jnp.float32, minval=-stdv, maxval=stdv)
        return {'x': x, 'adj': adj, 'weight': weight, 'bias': bias}
    _L1_gnn_all = _L1_gnn_setup()
    _L1_gnn_in = {k: v for k, v in _L1_gnn_all.items() if k in ('weight', 'bias')}
    del _L1_gnn_all

    def _L2_gnn_setup():
        import jax, jax.numpy as jnp
        import numpy as np
        B, N, D, C, L = (64, 256, 128, 128, 5)
        EDGE_P = 0.02

        def _gru_cell(m, h, w_ih, w_hh, b_ih, b_hh):
            gi = m @ w_ih.T + b_ih
            gh = h @ w_hh.T + b_hh
            i_r, i_z, i_n = jnp.split(gi, 3, axis=-1)
            h_r, h_z, h_n = jnp.split(gh, 3, axis=-1)
            r = jax.nn.sigmoid(i_r + h_r)
            z = jax.nn.sigmoid(i_z + h_z)
            n = jnp.tanh(i_n + r * h_n)
            return (1.0 - z) * n + z * h
        key = jax.random.key(seed)
        ks = jax.random.split(key, 8)
        x = jax.random.normal(ks[0], (B, N, D), dtype=jnp.float32)
        adj = (jax.random.uniform(ks[1], (B, N, N)) < EDGE_P).astype(jnp.float32)
        mask = jnp.ones((B, N), dtype=jnp.float32)
        s = 1.0 / np.sqrt(C).astype(np.float32)
        weight = jax.random.uniform(ks[2], (L, C, C), minval=-s, maxval=s, dtype=jnp.float32)
        w_ih = jax.random.uniform(ks[3], (3 * C, C), minval=-s, maxval=s, dtype=jnp.float32)
        w_hh = jax.random.uniform(ks[4], (3 * C, C), minval=-s, maxval=s, dtype=jnp.float32)
        b_ih = jax.random.uniform(ks[5], (3 * C,), minval=-s, maxval=s, dtype=jnp.float32)
        b_hh = jax.random.uniform(ks[6], (3 * C,), minval=-s, maxval=s, dtype=jnp.float32)
        return dict(x=x, adj=adj, mask=mask, weight=weight, w_ih=w_ih, w_hh=w_hh, b_ih=b_ih, b_hh=b_hh)
    _L2_gnn_all = _L2_gnn_setup()
    _L2_gnn_in = {k: v for k, v in _L2_gnn_all.items() if k in ('weight', 'w_ih', 'w_hh', 'b_ih', 'b_hh')}
    del _L2_gnn_all

    def _L3_gnn_setup():
        import jax, jax.numpy as jnp
        import numpy as np
        GROUPS = [list(range(25)), [0, 1, 2, 3, 4, 5, 6, 7, 8], [0, 9, 10, 11, 12, 13, 14], [6, 7, 8, 12, 13, 14], [3, 4, 5, 9, 10, 11]]
        B, N, D_IN, D_HID = (4096, 25, 128, 256)

        def _graph_conv(x, adj, W, b):
            n = adj.shape[-1]
            A = adj + jnp.eye(n, dtype=adj.dtype)
            deg = jnp.sum(A, axis=-1)
            deg_safe = jnp.where(deg == 0, 1.0, deg)
            dinv = jnp.where(deg == 0, 0.0, deg_safe ** (-0.5))
            norm_adj = dinv[:, :, None] * A * dinv[:, None, :]
            support = jnp.einsum('bnd,de->bne', x, W)
            out = jnp.einsum('bnm,bme->bne', norm_adj, support) + b
            return jax.nn.relu(out)
        key = jax.random.key(seed)
        ks = jax.random.split(key, 7)
        s1 = float(np.sqrt(6.0 / (D_IN + D_HID)))
        s2 = float(np.sqrt(6.0 / (D_HID + D_IN)))
        return {'x': jax.random.normal(ks[0], (B, N, D_IN), dtype=jnp.float32), 'adj': jax.random.uniform(ks[1], (B, N, N), dtype=jnp.float32), 'W1': jax.random.uniform(ks[2], (5, D_IN, D_HID), jnp.float32, -s1, s1), 'b1': jnp.zeros((5, D_HID), dtype=jnp.float32), 'W2': jax.random.uniform(ks[3], (5, D_HID, D_IN), jnp.float32, -s2, s2), 'b2': jnp.zeros((5, D_IN), dtype=jnp.float32), 'fusion_w': jnp.ones((5,), dtype=jnp.float32)}
    _L3_gnn_all = _L3_gnn_setup()
    _L3_gnn_in = {k: v for k, v in _L3_gnn_all.items() if k in ('W1', 'b1', 'W2', 'b2', 'fusion_w')}
    del _L3_gnn_all
    return {'x': x, 'adj': adj, 'nodemask': nodemask, 'L0_gnn_W': _L0_gnn_in['W'], 'L0_gnn_bias': _L0_gnn_in['bias'], 'L0_gnn_prelu_a': _L0_gnn_in['prelu_a'], 'L1_gnn_weight': _L1_gnn_in['weight'], 'L1_gnn_bias': _L1_gnn_in['bias'], 'L2_gnn_weight': _L2_gnn_in['weight'], 'L2_gnn_w_ih': _L2_gnn_in['w_ih'], 'L2_gnn_w_hh': _L2_gnn_in['w_hh'], 'L2_gnn_b_ih': _L2_gnn_in['b_ih'], 'L2_gnn_b_hh': _L2_gnn_in['b_hh'], 'L3_gnn_W1': _L3_gnn_in['W1'], 'L3_gnn_b1': _L3_gnn_in['b1'], 'L3_gnn_W2': _L3_gnn_in['W2'], 'L3_gnn_b2': _L3_gnn_in['b2'], 'L3_gnn_fusion_w': _L3_gnn_in['fusion_w']}

def reference(x, adj, nodemask, L0_gnn_W, L0_gnn_bias, L0_gnn_prelu_a, L1_gnn_weight, L1_gnn_bias, L2_gnn_weight, L2_gnn_w_ih, L2_gnn_w_hh, L2_gnn_b_ih, L2_gnn_b_hh, L3_gnn_W1, L3_gnn_b1, L3_gnn_W2, L3_gnn_b2, L3_gnn_fusion_w):
    import jax
    import jax.numpy as jnp

    def _L0_gnn_ref(seq, adj, W, bias, prelu_a):
        import jax, jax.numpy as jnp
        import numpy as np
        D_IN = 128
        D_OUT = 128
        seq_fts = jnp.einsum('bnd,de->bne', seq, W)
        out = jnp.einsum('bnm,bme->bne', adj, seq_fts) + bias
        return jnp.where(out >= 0, out, prelu_a * out)

    def _L1_gnn_ref(x, adj, weight, bias):
        import jax, jax.numpy as jnp
        import numpy as np
        support = jnp.einsum('bni,io->bno', x, weight)
        out = jnp.einsum('bnm,bmo->bno', adj, support)
        return out + bias

    def _L2_gnn_ref(x, adj, mask, weight, w_ih, w_hh, b_ih, b_hh):
        import jax, jax.numpy as jnp
        import numpy as np
        B, N, D, C, L = (64, 256, 128, 128, 5)
        EDGE_P = 0.02

        def _gru_cell(m, h, w_ih, w_hh, b_ih, b_hh):
            gi = m @ w_ih.T + b_ih
            gh = h @ w_hh.T + b_hh
            i_r, i_z, i_n = jnp.split(gi, 3, axis=-1)
            h_r, h_z, h_n = jnp.split(gh, 3, axis=-1)
            r = jax.nn.sigmoid(i_r + h_r)
            z = jax.nn.sigmoid(i_z + h_z)
            n = jnp.tanh(i_n + r * h_n)
            return (1.0 - z) * n + z * h
        A = (adj != 0).astype(x.dtype)
        h = x
        for l in range(weight.shape[0]):
            m = jnp.einsum('bnd,de->bne', h, weight[l])
            agg = jnp.einsum('bij,bid->bjd', A, m)
            h = _gru_cell(agg, h, w_ih, w_hh, b_ih, b_hh)
        return h * mask[..., None]

    def _L3_gnn_ref(x, adj, W1, b1, W2, b2, fusion_w):
        import jax, jax.numpy as jnp
        import numpy as np
        GROUPS = [list(range(25)), [0, 1, 2, 3, 4, 5, 6, 7, 8], [0, 9, 10, 11, 12, 13, 14], [6, 7, 8, 12, 13, 14], [3, 4, 5, 9, 10, 11]]
        B, N, D_IN, D_HID = (4096, 25, 128, 256)

        def _graph_conv(x, adj, W, b):
            n = adj.shape[-1]
            A = adj + jnp.eye(n, dtype=adj.dtype)
            deg = jnp.sum(A, axis=-1)
            deg_safe = jnp.where(deg == 0, 1.0, deg)
            dinv = jnp.where(deg == 0, 0.0, deg_safe ** (-0.5))
            norm_adj = dinv[:, :, None] * A * dinv[:, None, :]
            support = jnp.einsum('bnd,de->bne', x, W)
            out = jnp.einsum('bnm,bme->bne', norm_adj, support) + b
            return jax.nn.relu(out)
        norm_w = jax.nn.softmax(fusion_w)
        fused = jnp.zeros_like(x)
        for g, idx_list in enumerate(GROUPS):
            idx = jnp.asarray(idx_list)
            x_g = x[:, idx, :]
            adj_g = adj[:, idx][:, :, idx]
            h = _graph_conv(x_g, adj_g, W1[g], b1[g])
            out_g = _graph_conv(h, adj_g, W2[g], b2[g])
            fused = fused.at[:, idx, :].add(norm_w[g] * out_g)
        return fused
    x = _layernorm(x + _L0_gnn_ref(x, adj, L0_gnn_W, L0_gnn_bias, L0_gnn_prelu_a), axis=-1)
    x = _layernorm(x + _L1_gnn_ref(x, adj, L1_gnn_weight, L1_gnn_bias), axis=-1)
    x = _layernorm(x + _L2_gnn_ref(x, adj, nodemask, L2_gnn_weight, L2_gnn_w_ih, L2_gnn_w_hh, L2_gnn_b_ih, L2_gnn_b_hh), axis=-1)
    x = _layernorm(x + _L3_gnn_ref(x, adj, L3_gnn_W1, L3_gnn_b1, L3_gnn_W2, L3_gnn_b2, L3_gnn_fusion_w), axis=-1)
    return x

_drawn_inputs = setup_inputs


def setup_inputs(seed=0):
    import zlib

    import numpy as np

    out = dict(_drawn_inputs(seed))
    spreads = {'L0_gnn_bias': (0.0, 0.1),
     'L3_gnn_b1': (0.0, 0.8),
     'L3_gnn_b2': (0.0, 0.8),
     'L3_gnn_fusion_w': (1.0, 0.6)}
    factors = {}
    for name, (base, spread) in spreads.items():
        noise = np.random.default_rng([zlib.crc32(name.encode()), seed]).standard_normal(out[name].shape)
        drawn = base * np.exp(spread * noise) if base else spread * noise
        out[name] = jnp.asarray(drawn.astype(out[name].dtype))
    for name, factor in factors.items():
        out[name] = (out[name] * factor).astype(out[name].dtype)
    return out
```

```python
from contextlib import ExitStack

import concourse.bass as bass
from concourse import mybir

ALU = mybir.AluOpType
ACT = mybir.ActivationFunctionType
F32 = mybir.dt.float32
F32R = mybir.dt.float32r
F16 = mybir.dt.float16
AX_X = mybir.AxisListType.X

P = 128
EPS = 1e-5

RUNS = [[(0, 25)], [(0, 9)], [(0, 1), (9, 6)], [(6, 3), (12, 3)], [(3, 3), (9, 3)]]
SIZES = [sum(n for _, n in runs) for runs in RUNS]
OFFS = [sum(SIZES[:g]) for g in range(len(SIZES))]
SLOTS = sum(SIZES)
NODES = SIZES[0]
NG = len(RUNS)
SQ = [n * n for n in SIZES]
SQ_OFFS = [sum(SQ[:g]) for g in range(NG)]


def graph_stack_kernel(nc, x, adj, nodemask, w0, bias0, prelu_a, w1, bias1, gw, w_ih, w_hh,
                       b_ih, b_hh, l3_w1, l3_b1, l3_w2, l3_b2, fusion_w, out):
    B, N, D = x.shape
    L = gw.shape[0]
    G4 = 4
    STEPS_A = B // G4
    ITERS = B // (2 * G4)
    G8 = 8
    STEPS_C = B // G8
    GATE = 3 * D
    HC = l3_w1.shape[2] // P
    SL8 = G8 * SLOTS
    SMALL = 6 + NG + NG * HC
    assert N == P and D == P

    an_dram = nc.dram_tensor("an_dram", (B, sum(SQ)), F32, kind="Internal").ap()
    adj_nm = adj.rearrange("s n m -> n s m")
    x_nm = x.rearrange("s n d -> n s d")
    out_nm = out.rearrange("s n d -> n s d")

    ctx = ExitStack()
    with ctx:
        def sem(name):
            return ctx.enter_context(nc.semaphore(name))

        def sb(name, shape, dt=F32, scope=ctx):
            return scope.enter_context(nc.sbuf_tensor(name, shape, dt))

        x2 = sb("x2", [P, B * D])
        ident = sb("ident", [P, P])
        w0_sb = sb("w0_sb", [P, D])
        w1_sb = sb("w1_sb", [P, D])
        bias0_bc = sb("bias0_bc", [P, D])
        bias1_bc = sb("bias1_bc", [P, D])
        alpha = sb("alpha", [P, 1])
        smallT = sb("smallT", [P, SMALL])
        bih, bhh = smallT[:, 0:3], smallT[:, 3:6]
        b2T, b1T = smallT[:, 6:6 + NG], smallT[:, 6 + NG:SMALL]
        nbz = sb("nbz", [P, 1])
        brz = sb("brz", [P, 2])
        maskT = sb("maskT", [P, B])
        half = sb("half", [P, G8])
        eps = sb("eps", [P, G8])
        wx_hi = sb("wx_hi", [P, L * GATE], F32R)
        wx_lo = sb("wx_lo", [P, L * GATE], F32R)
        wh_hi = sb("wh_hi", [P, GATE], F32R)
        wh_lo = sb("wh_lo", [P, GATE], F32R)
        v1 = sb("v1", [P, NG * HC * P])
        v2 = sb("v2", [P, NG * HC * P])
        nw = sb("nw", [P, NG])
        nwb2 = sb("nwb2", [P, NG])
        anT = sb("anT", [P, sum(SQ)])

        bank = [ctx.enter_context(nc.psum_tensor(f"bank{i}", [P, 512], F32)) for i in range(6)]
        bank67 = ctx.enter_context(nc.psum_tensor("bank67", [P, 1024], F32))
        bank += [bank67[:, 0:512], bank67[:, 512:1024]]

        sa = ExitStack()
        sc_raw = sb("wraw", [P, (2 * 3 + L) * P], scope=sa)
        wT = sb("wT", [P, (3 + L) * P], scope=sa)
        mask_sb = sb("mask_sb", [P, P], scope=sa)
        small = sb("small", [SMALL, P], scope=sa)
        fw = sb("fw", [P, NG], scope=sa)
        fmx = sb("fmx", [P, 1], scope=sa)
        fsum = sb("fsum", [P, 1], scope=sa)
        adj25 = sb("adj25", [P, NODES * NODES], scope=sa)
        cmp_a = sb("cmp_a", [P, sum(SQ)], scope=sa)
        deg = sb("deg", [P, SLOTS], scope=sa)
        deg0 = sb("deg0", [P, SLOTS], scope=sa)
        dinv = sb("dinv", [P, SLOTS], scope=sa)
        half53 = sb("half53", [P, SLOTS], scope=sa)

        ADJ = [sb(f"adj{i}", [P, G4 * N], scope=sa) for i in range(4)]
        X0 = [sb(f"x0_{i}", [P, G4 * D], scope=sa) for i in range(4)]
        ADJT = [sb(f"adjT{i}", [P, G4 * N], scope=sa) for i in range(4)]
        X1 = [sb(f"x1_{i}", [P, G4 * D], scope=sa) for i in range(4)]
        YT0 = sb("yT0", [P, G4 * N], scope=sa)
        YT1 = sb("yT1", [P, G4 * N], scope=sa)
        U = sb("u", [P, G4 * D], scope=sa)
        V = sb("v", [P, G4 * D], scope=sa)
        WS0 = [sb(f"ws0_{i}", [P, G4 * D], scope=sa) for i in range(2)]
        WS1 = [sb(f"ws1_{i}", [P, G4 * D], scope=sa) for i in range(2)]
        X1B = [sb(f"x1b{i}", [P, G4 * D], scope=sa) for i in range(2)]
        ST0, ST1 = (sb(f"st{i}", [P, G4 * 6], scope=sa) for i in range(2))
        MV0 = [sb(f"mv0_{i}", [P, G4 * 2], scope=sa) for i in range(2)]
        MV1 = [sb(f"mv1_{i}", [P, G4 * 2], scope=sa) for i in range(2)]
        VE0, VE1 = (sb(f"ve{i}", [P, G4], scope=sa) for i in range(2))
        RS0 = [sb(f"rs0_{i}", [P, G4], scope=sa) for i in range(2)]
        RS1 = [sb(f"rs1_{i}", [P, G4], scope=sa) for i in range(2)]
        sa.close()

        mt = sb("mt", [P, B * SLOTS])
        n2 = sb("n2", [P, B // 2 * 2 * SLOTS])
        sbb = ExitStack()
        ADJR = [sb(f"adjr{s}", [P, G4 * N], scope=sbb) for s in range(2)]
        A16 = [sb(f"a16_{s}", [P, G4 * N], F16, scope=sbb) for s in range(2)]
        X2S = [sb(f"x2s{s}", [P, G4 * D], scope=sbb) for s in range(2)]
        HT = [sb(f"ht{s}", [P, G4 * N], scope=sbb) for s in range(2)]
        HT_HI = [sb(f"hth{s}", [P, G4 * N], F32R, scope=sbb) for s in range(2)]
        HT_LO = [sb(f"htl{s}", [P, G4 * N], F32R, scope=sbb) for s in range(2)]
        PT_HI = [sb(f"pth{s}", [P, G4 * N], F32R, scope=sbb) for s in range(2)]
        PT_LO = [sb(f"ptl{s}", [P, G4 * N], F32R, scope=sbb) for s in range(2)]
        HN_HI = [sb(f"hnh{s}", [P, G4 * D], F16, scope=sbb) for s in range(2)]
        HN_LO = [sb(f"hnl{s}", [P, G4 * D], F16, scope=sbb) for s in range(2)]
        RT = [sb(f"rt{s}", [P, G4 * N], scope=sbb) for s in range(2)]
        ZW = [sb(f"zw{s}", [P, G4 * N], scope=sbb) for s in range(2)]
        ZH = [sb(f"zh{s}", [P, G4 * N], scope=sbb) for s in range(2)]
        WB = [sb(f"wb{s}", [P, G4 * N], scope=sbb) for s in range(2)]
        YB = [sb(f"yb{s}", [P, G4 * D], scope=sbb) for s in range(2)]
        STB = [sb(f"stb{s}", [P, G4 * 6], scope=sbb) for s in range(2)]
        MVB = [sb(f"mvb{s}", [P, G4 * 2], scope=sbb) for s in range(2)]
        VEB = [sb(f"veb{s}", [P, G4], scope=sbb) for s in range(2)]
        RSB = [sb(f"rsb{s}", [P, G4], scope=sbb) for s in range(2)]
        sbb.close()

        X3S = sb("x3s", [P, G8 * D])
        SP_T = sb("sp_t", [P, SL8])
        HID = [sb(f"hid{c}", [P, SL8]) for c in range(HC)]
        TT = sb("tt", [P, SL8])
        TN = sb("tn", [P, G8 // 2 * P])
        OT = sb("ot", [P, SL8])
        YO = sb("yo", [P, 2 * G8 * D])
        STC = sb("stc", [P, G8 * 6])
        MVC = sb("mvc", [P, 2 * G8 * 2])
        VEC = sb("vec", [P, G8])
        RSC = sb("rsc", [P, 2 * G8])

        w_ld_tr = sem("w_ld_tr")
        w_ld_a25 = sem("w_ld_a25")
        w_ld_fw = sem("w_ld_fw")
        w_ld_misc = sem("w_ld_misc")
        w_ident = sem("w_ident")
        w_consts = sem("w_consts")
        w_tr = sem("w_tr")
        w_ev = sem("w_ev")
        w_prod = sem("w_prod")
        w_hi = sem("w_hi")
        w_lo = sem("w_lo")
        w_v = sem("w_v")
        w_exp = sem("w_exp")
        w_pow = sem("w_pow")
        an_st = sem("an_st")
        n2_zero = sem("n2_zero")
        l3_ld = sem("l3_ld")

        a_ld = [sem(f"a_ld{i}") for i in range(4)]
        a_tadj = sem("a_tadj")
        a_adjT = sem("a_adjT")
        a_y0, a_yT0, a_z0 = sem("a_y0"), sem("a_yT0"), sem("a_z0")
        a_y1, a_yT1, a_z1 = sem("a_y1"), sem("a_yT1"), sem("a_z1")
        a_u, a_m, a_v, a_w0 = sem("a_u"), sem("a_m"), sem("a_v"), sem("a_w0")
        a_w1 = sem("a_w1")
        a_bs0, a_mv0, a_ve0, a_rs0 = sem("a_bs0"), sem("a_mv0"), sem("a_ve0"), sem("a_rs0")
        a_bs1, a_mv1, a_ve1, a_rs1 = sem("a_bs1"), sem("a_mv1"), sem("a_ve1"), sem("a_rs1")
        a_x1, a_x1b, a_x2 = sem("a_x1"), sem("a_x1b"), sem("a_x2")

        def sem2(name):
            return [sem(f"{name}{s}") for s in range(2)]

        b_ldx, b_lda, b_a16 = sem2("b_ldx"), sem2("b_lda"), sem2("b_a16")
        b_t0, b_h0 = sem2("b_t0"), sem2("b_h0")
        b_hnh, b_hnl, b_hth, b_htl = sem2("b_hnh"), sem2("b_hnl"), sem2("b_hth"), sem2("b_htl")
        b_at, b_ph, b_pl = sem2("b_at"), sem2("b_ph"), sem2("b_pl")
        b_R, b_I, b_Z = sem2("b_R"), sem2("b_I"), sem2("b_Z")
        b_r, b_t1, b_t2, b_z, b_n = sem2("b_r"), sem2("b_t1"), sem2("b_t2"), sem2("b_z"), sem2("b_n")
        b_zh, b_w, b_q, b_h, b_tp = sem2("b_zh"), sem2("b_w"), sem2("b_q"), sem2("b_h"), sem2("b_tp")
        b_ye, b_ym = sem2("b_ye"), sem2("b_ym")
        b_y, b_bs, b_mv, b_ve, b_rs, b_x3 = (sem2("b_y"), sem2("b_bs"), sem2("b_mv"), sem2("b_ve"),
                                             sem2("b_rs"), sem2("b_x3"))

        c_ldx, c_s, c_st = sem("c_ldx"), sem("c_s"), sem("c_st")
        c_h = [sem(f"c_h{c}") for c in range(HC)]
        c_rh = [sem(f"c_rh{c}") for c in range(HC)]
        c_t, c_tt, c_n, c_tn = sem("c_t"), sem("c_tt"), sem("c_n"), sem("c_tn")
        c_o, c_ro, c_add, c_f = sem("c_o"), sem("c_ro"), sem("c_add"), sem("c_f")
        c_x, c_bs, c_mv, c_ve, c_rs, c_yo = (sem("c_x"), sem("c_bs"), sem("c_mv"), sem("c_ve"),
                                             sem("c_rs"), sem("c_yo"))
        c_out = [sem(f"c_out{i}") for i in range(2)]

        block = ctx.enter_context(nc.Block())

        def steps_a(role):
            last_lag = 4
            total = STEPS_A + last_lag

            def peeled(k):
                role(k, k % 4, lambda lag: 0 <= k - lag < STEPS_A)
            return peeled, total

        def run_a(eng, role):
            peeled, total = steps_a(role)
            for k in range(4):
                peeled(k)
            with eng.Fori(1, STEPS_A // 4) as j:
                for m in range(4):
                    role(j * 4 + m, m, lambda lag: True)
            for k in range(STEPS_A, total):
                peeled(k)

        items = [(s, l) for l in range(L) for s in range(2)]

        def run_b(eng, half_step):
            def item(i, it):
                n = len(items)
                at = it + i // n
                if isinstance(at, int) and not 0 <= at < ITERS:
                    return None
                return (*items[i % n], at)

            def half(j, it):
                second = item(j, it)
                tails = [t if t and t[1] == L - 1 else None for t in (item(j - 1, it), item(j - 2, it), item(j - 3, it))]
                after = item(j + 2, it) if second and second[1] == L - 1 else None
                half_step(item(j + 1, it), second, tails, after)

            def body(it):
                for j in range(len(items)):
                    half(j, it)
            half_step(item(0, 0), None, [None] * 3, item(1, 0))
            body(0)
            with eng.Fori(1, ITERS - 1) as it:
                body(it)
            body(ITERS - 1)
            for j in range(3):
                half(len(items) + j, ITERS - 1)

        def run_c(eng, step):
            for k in range(4):
                step(k, k % 2, lambda lag: k - lag >= 0)
            with eng.Fori(2, STEPS_C // 2) as j:
                for m in range(2):
                    step(j * 2 + m, m, lambda lag: True)
            for k in range(STEPS_C, STEPS_C + 2):
                step(k, k % 2, lambda lag: k - lag < STEPS_C)

        def wait_apart(eng, signal, value):
            eng.wait_ge(w_ident, 2)
            eng.wait_ge(signal, value)

        def cols(t, i):
            return t[:, i * P:(i + 1) * P]

        def bc4(t):
            return t[:, :].unsqueeze(1).to_broadcast([P, G4, D])

        def v4(t):
            return t.rearrange("p (s d) -> p s d", s=G4)

        @block.sync
        def _(sp):
            sp.dma_start(sc_raw[:, 0:3 * P].rearrange("p (g d) -> p g d", g=3),
                         w_ih.rearrange("(g p) d -> p g d", p=P)).then_inc(w_ld_tr, 16)
            sp.dma_start(sc_raw[:, 3 * P:6 * P].rearrange("p (g d) -> p g d", g=3),
                         w_hh.rearrange("(g p) d -> p g d", p=P)).then_inc(w_ld_tr, 16)
            sp.dma_start(sc_raw[:, 6 * P:(6 + L) * P].rearrange("p (g d) -> p g d", g=L),
                         gw.rearrange("l p d -> p l d")).then_inc(w_ld_tr, 16)
            sp.dma_start(mask_sb[:, :], nodemask).then_inc(w_ld_tr, 16)
            sp.dma_start(small[0:3, :], b_ih.rearrange("(g p) -> g p", p=P)).then_inc(w_ld_tr, 16)
            sp.dma_start(small[3:6, :], b_hh.rearrange("(g p) -> g p", p=P)).then_inc(w_ld_tr, 16)
            sp.dma_start(small[6:6 + NG, :], l3_b2).then_inc(w_ld_tr, 16)
            sp.dma_start(small[6 + NG:SMALL, :], l3_b1.rearrange("g (c p) -> (g c) p", p=P)).then_inc(w_ld_tr, 16)
            sp.dma_start(w0_sb[:, :], w0).then_inc(w_ld_misc, 16)
            sp.dma_start(w1_sb[:, :], w1).then_inc(w_ld_misc, 16)
            sp.dma_start(bias0_bc[:, :], bias0.partition_broadcast(P)).then_inc(w_ld_misc, 16)
            sp.dma_start(bias1_bc[:, :], bias1.partition_broadcast(P)).then_inc(w_ld_misc, 16)
            sp.dma_start(alpha[:, :], prelu_a.partition_broadcast(P)).then_inc(w_ld_misc, 16)

            def load_a(k, m, has):
                if not has(0):
                    return
                if not (isinstance(k, int) and k < 4):
                    sp.wait_ge(a_w0, k - 3)
                sp.dma_start(v4(ADJ[m][:, :]), adj_nm[:, bass.ds(k * G4, G4), :]).then_inc(a_ld[m], 16)
                sp.dma_start(v4(X0[m][:, :]), x_nm[:, bass.ds(k * G4, G4), :]).then_inc(a_ld[m], 16)
            for k in range(4):
                load_a(k, k, lambda lag: True)
            sp.dma_start(adj25[:, :].rearrange("s (i j) -> s i j", i=NODES),
                         adj[:, 0:NODES, 0:NODES]).then_inc(w_ld_a25, 16)
            sp.dma_start(fw[:, :], fusion_w.partition_broadcast(P)).then_inc(w_ld_fw, 16)
            sp.dma_start(v1[:, :].rearrange("p (g e) -> p g e", g=NG),
                         l3_w1.rearrange("g p e -> p g e")).then_inc(w_ld_misc, 16)
            sp.dma_start(v2[:, :].rearrange("p (g c d) -> p g c d", g=NG, c=HC),
                         l3_w2.rearrange("g (c p) d -> p g c d", p=P)).then_inc(w_ld_misc, 16)
            with sp.Fori(1, STEPS_A // 4) as j:
                for m in range(4):
                    load_a(j * 4 + m, m, lambda lag: True)

            def load_b(s, it):
                if not (isinstance(it, int) and it == 0):
                    sp.wait_ge(b_t0[s], it)
                    sp.wait_ge(b_hnl[s], L * it - (L - 1))
                    sp.wait_ge(b_a16[s], it)
                q = it * 2 + s
                sp.dma_start(X2S[s][:, :], x2[:, bass.ds(q * G4 * D, G4 * D)]).then_inc(b_ldx[s], 16)
                sp.dma_start(v4(ADJR[s][:, :]), adj_nm[:, bass.ds(q * G4, G4), :]).then_inc(b_lda[s], 16)
            sp.wait_ge(w_v, W_AN)
            sp.dma_start(an_dram, anT[:, :]).then_inc(an_st, 16)
            sp.wait_ge(a_x2, STEPS_A)
            for s in range(2):
                load_b(s, 0)
            sp.wait_ge(n2_zero, 4)
            sp.wait_ge(an_st, 16)
            n2v = n2[:, :].rearrange("p (q c) -> p q c", c=2 * SLOTS)
            mtv = mt[:, :].rearrange("p (s c) -> p s c", c=SLOTS)
            an = [an_dram[:, SQ_OFFS[g]:SQ_OFFS[g] + SQ[g]].rearrange("s (j i) -> j s i", i=SIZES[g])
                  for g in range(NG)]
            for g in range(NG):
                at = 0
                for m0, cnt in RUNS[g]:
                    sp.dma_start(mtv[m0:m0 + cnt, :, OFFS[g]:OFFS[g] + SIZES[g]], an[g][at:at + cnt, :, :])\
                      .then_inc(l3_ld, 16)
                    at += cnt
                for par in range(2):
                    r = par * SLOTS + OFFS[g]
                    sp.dma_start(n2v[r:r + SIZES[g], :, r:r + SIZES[g]], an[g][:, par:B:2, :])\
                      .then_inc(l3_ld, 16)
            with sp.Fori(1, ITERS) as it:
                for s in range(2):
                    load_b(s, it)

            def step_c(k, m, has):
                if has(0):
                    if isinstance(k, int) and k == 0:
                        for s in range(2):
                            sp.wait_ge(b_x3[s], ITERS)
                    else:
                        sp.wait_ge(c_s, k)
                    sp.dma_start(X3S[0:NODES, :], x2[0:NODES, bass.ds(k * G8 * D, G8 * D)])\
                      .then_inc(c_ldx, 16)
                if has(2):
                    sp.wait_ge(c_yo, k - 1)
                    sp.dma_start(out_nm[:, bass.ds((k - 2) * G8, G8), :],
                                 YO[:, m * G8 * D:(m + 1) * G8 * D].rearrange("p (s d) -> p s d", s=G8))\
                      .then_inc(c_out[m], 16)
            run_c(sp, step_c)
            for i in range(2):
                sp.wait_ge(c_out[i], 16 * (STEPS_C // 2))

        @block.gpsimd
        def _(pool):
            nc.gpsimd.memset(ident[:, :], 0.0).then_inc(w_ident, 1)
            pool.wait_ge(w_ident, 1)
            nc.gpsimd.affine_select(out=ident[:, :], in_=ident[:, :], compare_op=ALU.not_equal, fill=1.0,
                                    base=0, pattern=[[-1, P]], channel_multiplier=1).then_inc(w_ident, 1)
            nc.gpsimd.memset(half[:, :], -0.5).then_inc(w_consts, 1)
            nc.gpsimd.memset(half53[:, :], -0.5).then_inc(w_consts, 1)
            nc.gpsimd.memset(eps[:, :], EPS).then_inc(w_consts, 1)
            pool.wait_ge(w_consts, 3)
            pool.wait_ge(w_v, W_DEG)
            nc.gpsimd.tensor_tensor(dinv[:, :], deg[:, :], half53[:, :], ALU.pow).then_inc(w_pow, 1)

            def rstd(mv, ve, rs, n, s_mv, at, s_ve, s_rs):
                pool.wait_ge(s_mv, at)
                nc.gpsimd.tensor_tensor(ve[:, :], mv.rearrange("p (s t) -> p s t", t=2)[:, :, 1],
                                        eps[:, 0:n], ALU.add).then_inc(s_ve, 1)
                pool.wait_ge(s_ve, at)
                nc.gpsimd.tensor_tensor(rs, ve[:, :], half[:, 0:n], ALU.pow).then_inc(s_rs, 1)

            def step_a(k, m, has):
                if has(2):
                    pool.wait_ge(a_x1, k - 1)
                    nc.gpsimd.tensor_tensor(v4(X1B[m % 2][:, :]), v4(X1[(m - 2) % 4][:, :]),
                                            bc4(bias1_bc), ALU.add).then_inc(a_x1b, 1)
                if has(1):
                    rstd(MV0[(m - 1) % 2][:, :], VE0, RS0[(m - 1) % 2][:, :], G4, a_mv0, k, a_ve0, a_rs0)
                if has(3):
                    rstd(MV1[(m - 3) % 2][:, :], VE1, RS1[(m - 3) % 2][:, :], G4, a_mv1, k - 2, a_ve1, a_rs1)
            pool.wait_ge(w_ld_misc, 16 * 7)
            run_a(pool, step_a)

            pool.wait_ge(a_x2, STEPS_A)
            for h in range(2):
                w = B // 2 * SLOTS
                nc.gpsimd.memset(n2[:, h * w:(h + 1) * w], 0.0).then_inc(n2_zero, 1)
                nc.gpsimd.memset(mt[:, h * w:(h + 1) * w], 0.0).then_inc(n2_zero, 1)

            def half_b(first, second, tails, after):
                if first:
                    s, l, it = first
                    n1 = it * L + l + 1
                    pool.wait_ge(b_hth[s], n1)
                    if l == 0:
                        pool.wait_ge(b_h0[s], it + 1)
                    nc.gpsimd.tensor_tensor(HT_LO[s][:, :], HT[s][:, :], HT_HI[s][:, :].bitcast(F32),
                                            ALU.subtract).then_inc(b_htl[s], 1)
                if second:
                    s, l, it = second
                    n1 = it * L + l + 1
                    pool.wait_ge(b_z[s], n1)
                    nc.gpsimd.tensor_tensor(ZH[s][:, :], ZW[s][:, :], HT[s][:, :], ALU.mult)\
                      .then_inc(b_zh[s], 1)
                if tails[0]:
                    s, l, it = tails[0]
                    q = it * 2 + s
                    wait_apart(pool, b_ye[s], it + 1)
                    nc.gpsimd.tensor_tensor(v4(YB[s][:, :]), v4(YB[s][:, :]),
                                            maskT[:, bass.ds(q * G4, G4)].unsqueeze(2).to_broadcast([P, G4, D]),
                                            ALU.mult).then_inc(b_ym[s], 1)
                    wait_apart(pool, b_ym[s], it + 1)
                    nc.gpsimd.tensor_tensor(YB[s][:, :], YB[s][:, :], x2[:, bass.ds(q * G4 * D, G4 * D)],
                                            ALU.add).then_inc(b_y[s], 1)
                if tails[1]:
                    s, l, it = tails[1]
                    rstd(MVB[s][:, :], VEB[s], RSB[s][:, :], G4, b_mv[s], it + 1, b_ve[s], b_rs[s])
            run_b(pool, half_b)

            def step_c(k, m, has):
                if has(2):
                    rstd(MVC[:, m * G8 * 2:(m + 1) * G8 * 2], VEC, RSC[:, m * G8:(m + 1) * G8], G8,
                         c_mv, k - 1, c_ve, c_rs)
            run_c(pool, step_c)

        @block.scalar
        def _(act):
            act.wait_ge(w_tr, 1)
            nc.scalar.activation(maskT[:, :], bank[5][:, 0:P], ACT.Copy).then_inc(w_ev, 1)
            nc.scalar.activation(wT[:, 0:3 * P], bank[6][:, 0:3 * P], ACT.Copy).then_inc(w_ev, 1)
            nc.scalar.activation(wT[:, 3 * P:7 * P], bank[4][:, :], ACT.Copy).then_inc(w_ev, 1)
            nc.scalar.activation(wT[:, 7 * P:8 * P], bank[5][:, P:2 * P], ACT.Copy).then_inc(w_ev, 1)
            nc.scalar.activation(smallT[:, :], bank[5][:, 2 * P:2 * P + SMALL], ACT.Copy).then_inc(w_ev, 1)
            nc.scalar.activation(wh_hi[:, :], bank[7][:, 0:3 * P], ACT.Copy).then_inc(w_hi, 1)
            for l in range(L):
                act.wait_ge(w_prod, l + 1)
                nc.scalar.activation(wx_hi[:, l * GATE:(l + 1) * GATE], bank[l][:, 0:GATE], ACT.Copy)\
                  .then_inc(w_hi, 1)
            act.wait_ge(w_v, W_FMX)
            nc.scalar.activation(fw[:, :], fw[:, :], ACT.Exp, bias=fmx[:, 0:1], accum_out=fsum[:, 0:1])\
              .then_inc(w_exp, 1)

            def step_a(k, m, has):
                if has(0):
                    act.wait_ge(a_tadj, k + 1)
                    if has(4):
                        act.wait_ge(a_y1, k - 3)
                    nc.scalar.activation(ADJT[m][:, :], bank[0][:, :], ACT.Copy).then_inc(a_adjT, 1)
                if has(2):
                    act.wait_ge(a_y1, k - 1)
                    nc.scalar.activation(YT1[:, :], bank[3][:, :], ACT.Copy).then_inc(a_yT1, 1)
                if has(0):
                    act.wait_ge(a_y0, k + 1)
                    nc.scalar.activation(YT0[:, :], bank[1][:, :], ACT.Copy).then_inc(a_yT0, 1)
            run_a(act, step_a)

            def half_b(first, second, tails, after):
                if second:
                    s, l, it = second
                    n1 = it * L + l + 1
                    act.wait_ge(b_R[s], n1)
                    nc.scalar.activation(RT[s][:, :], bank[4 * s + 0][:, :], ACT.Sigmoid,
                                         bias=brz[:, 0:1]).then_inc(b_r[s], 1)
                if first:
                    s, l, it = first
                    n1 = it * L + l + 1
                    if l == 0:
                        act.wait_ge(b_t0[s], it + 1)
                        nc.scalar.activation(HT_HI[s][:, :], bank[4 * s + 2][:, :], ACT.Copy)\
                          .then_inc(b_hth[s], 1)
                        act.wait_ge(b_ldx[s], 16 * it + 16)
                        nc.scalar.activation(HN_HI[s][:, :], X2S[s][:, :], ACT.Copy).then_inc(b_hnh[s], 1)
                    else:
                        act.wait_ge(b_h[s], n1 - 1)
                        nc.scalar.activation(HT_HI[s][:, :], HT[s][:, :], ACT.Copy).then_inc(b_hth[s], 1)
                if tails[0]:
                    s, l, it = tails[0]
                    act.wait_ge(b_tp[s], it * L + L)
                    nc.scalar.activation(YB[s][:, :], bank[4 * s + 3][:, :], ACT.Copy).then_inc(b_ye[s], 1)
                if first:
                    s, l, it = first
                    n1 = it * L + l + 1
                    if l > 0:
                        act.wait_ge(b_tp[s], n1 - 1)
                        nc.scalar.activation(HN_HI[s][:, :], bank[4 * s + 3][:, :], ACT.Copy)\
                          .then_inc(b_hnh[s], 1)
                if second:
                    s, l, it = second
                    n1 = it * L + l + 1
                    act.wait_ge(b_Z[s], n1)
                    nc.scalar.activation(ZW[s][:, :], bank[4 * s + 1][:, :], ACT.Sigmoid,
                                         bias=brz[:, 1:2]).then_inc(b_z[s], 1)
                    nc.scalar.activation(WB[s][:, :], bank[4 * s + 1][:, :], ACT.Sigmoid,
                                         bias=nbz[:, 0:1], scale=-1.0).then_inc(b_w[s], 1)
                    act.wait_ge(b_t2[s], n1)
                    nc.scalar.activation(RT[s][:, :], RT[s][:, :], ACT.Tanh, bias=bih[:, 2:3])\
                      .then_inc(b_n[s], 1)
                if first:
                    s, l, it = first
                    n1 = it * L + l + 1
                    act.wait_ge(b_at[s], n1)
                    nc.scalar.activation(PT_HI[s][:, :], bank[4 * s + 3][:, :], ACT.Copy)\
                      .then_inc(b_ph[s], 1)
            act.wait_ge(w_v, W_BRZ)
            act.wait_ge(a_x2, STEPS_A)
            run_b(act, half_b)

            def sl(t, g):
                return t.rearrange("p (s c) -> p s c", c=SLOTS)[:, :, OFFS[g]:OFFS[g] + SIZES[g]]

            def step_c(k, m, has):
                if has(1):
                    act.wait_ge(c_n, k)
                    nc.scalar.activation(TN[0:2 * SLOTS, :], bank[4][0:2 * SLOTS, :], ACT.Copy)\
                      .then_inc(c_tn, 1)
                if has(0):
                    act.wait_ge(c_s, k + 1)
                    nc.scalar.activation(SP_T[:, :], bank[0][:, 0:SL8], ACT.Copy).then_inc(c_st, 1)
                if has(1):
                    act.wait_ge(c_o, k)
                    for g in range(NG):
                        nc.scalar.activation(sl(OT[:, :], g), sl(bank[5][:, 0:SL8], g), ACT.Relu,
                                             bias=nwb2[:, g:g + 1], scale=nw[:, g:g + 1]).then_inc(c_ro, 1)
                if has(0):
                    act.wait_ge(c_h[0], k + 1)
                    for g in range(NG):
                        nc.scalar.activation(sl(HID[0][:, :], g), sl(bank[1][:, 0:SL8], g), ACT.Relu,
                                             bias=b1T[:, g * HC:g * HC + 1]).then_inc(c_rh[0], 1)
                    act.wait_ge(c_t, k + 1)
                    nc.scalar.activation(TT[:, :], bank[3][:, 0:SL8], ACT.Copy).then_inc(c_tt, 1)
            for s in range(2):
                act.wait_ge(b_x3[s], ITERS)
            run_c(act, step_c)

        @block.vector
        def _(dve):
            def norm(tile, st, mv, n, s_in, at, s_bs, s_mv):
                wait_apart(dve, s_in, at)
                for i in range(n):
                    last = nc.vector.bn_stats(st[:, 6 * i:6 * i + 6], tile[:, i * D:(i + 1) * D])
                last.then_inc(s_bs, 1)
                wait_apart(dve, s_bs, at)
                for i in range(n):
                    last = nc.vector.bn_aggr(mv[:, 2 * i:2 * i + 2], st[:, 6 * i:6 * i + 6])
                last.then_inc(s_mv, 1)

            def apply(dst, tile, mv, rs, n, s_rs, at, s_out):
                dve.wait_ge(s_rs, at)
                for i in range(n):
                    last = nc.vector.tensor_scalar(dst(i), tile[:, i * D:(i + 1) * D], mv[:, 2 * i:2 * i + 1],
                                                   rs[:, i:i + 1], ALU.subtract, ALU.mult)
                last.then_inc(s_out, 1)

            dve.wait_ge(w_hi, 1)
            nc.vector.tensor_tensor(wh_lo[:, :], bank[7][:, 0:3 * P], wh_hi[:, :].bitcast(F32),
                                    ALU.subtract).then_inc(w_lo, 1)
            for l in range(L):
                dve.wait_ge(w_hi, l + 2)
                sl = slice(l * GATE, (l + 1) * GATE)
                nc.vector.tensor_tensor(wx_lo[:, sl], bank[l][:, 0:GATE], wx_hi[:, sl].bitcast(F32),
                                        ALU.subtract).then_inc(w_lo, 1)

            count = [0]

            def link(ins):
                count[0] += 1
                ins.then_inc(w_v, 1)
                dve.wait_ge(w_v, count[0])

            dve.wait_ge(w_ld_fw, 16)
            dve.wait_ge(w_ev, 5)
            link(nc.vector.tensor_tensor(brz[:, :], bih[:, 0:2], bhh[:, 0:2], ALU.add))
            link(nc.vector.tensor_scalar(nbz[:, :], brz[:, 1:2], -1.0, None, ALU.mult))
            link(nc.vector.tensor_reduce(fmx[:, :], fw[:, :], AX_X, ALU.max))
            link(nc.vector.tensor_scalar(fmx[:, :], fmx[:, :], -1.0, None, ALU.mult))
            dve.wait_ge(w_ld_a25, 16)
            link(nc.vector.tensor_scalar(adj25[:, 0:NODES * NODES:NODES + 1],
                                         adj25[:, 0:NODES * NODES:NODES + 1], 1.0, None, ALU.add))
            a25 = adj25[:, :].rearrange("s (i j) -> s i j", i=NODES)
            ca = [cmp_a[:, SQ_OFFS[g]:SQ_OFFS[g] + SQ[g]].rearrange("s (i j) -> s i j", i=SIZES[g])
                  for g in range(NG)]
            for g in range(NG):
                r0 = 0
                for i0, ni in RUNS[g]:
                    c0 = 0
                    for j0, nj in RUNS[g]:
                        last = nc.vector.tensor_copy(ca[g][:, r0:r0 + ni, c0:c0 + nj],
                                                     a25[:, i0:i0 + ni, j0:j0 + nj])
                        c0 += nj
                    r0 += ni
            link(last)
            for g in range(NG):
                last = nc.vector.tensor_reduce(deg[:, OFFS[g]:OFFS[g] + SIZES[g]], ca[g], AX_X, ALU.add)
            link(last)
            link(nc.vector.tensor_scalar(deg0[:, :], deg[:, :], 0.0, None, ALU.is_equal))
            link(nc.vector.tensor_tensor(deg[:, :], deg[:, :], deg0[:, :], ALU.add))
            link(nc.vector.tensor_scalar(deg0[:, :], deg0[:, :], -1.0, 1.0, ALU.mult, ALU.add))
            dve.wait_ge(w_pow, 1)
            link(nc.vector.tensor_tensor(dinv[:, :], dinv[:, :], deg0[:, :], ALU.mult))
            an = [anT[:, SQ_OFFS[g]:SQ_OFFS[g] + SQ[g]].rearrange("s (j i) -> s j i", i=SIZES[g])
                  for g in range(NG)]
            for g in range(NG):
                d = dinv[:, OFFS[g]:OFFS[g] + SIZES[g]]
                last = nc.vector.tensor_tensor(an[g], ca[g].rearrange("s i j -> s j i"),
                                               d.unsqueeze(1).to_broadcast([P, SIZES[g], SIZES[g]]), ALU.mult)
            link(last)
            for g in range(NG):
                d = dinv[:, OFFS[g]:OFFS[g] + SIZES[g]]
                last = nc.vector.tensor_tensor(an[g], an[g],
                                               d.unsqueeze(2).to_broadcast([P, SIZES[g], SIZES[g]]), ALU.mult)
            link(last)
            dve.wait_ge(w_exp, 1)
            link(nc.vector.reciprocal(fsum[:, :], fsum[:, :]))
            link(nc.vector.tensor_scalar(nw[:, :], fw[:, :], fsum[:, 0:1], None, ALU.mult))
            link(nc.vector.tensor_tensor(nwb2[:, :], nw[:, :], b2T[:, :], ALU.mult))
            assert count[0] == W_ALL
            dve.wait_ge(w_ld_misc, 16 * 7)

            def step_a(k, m, has):
                if has(2):
                    p = m % 2
                    apply(lambda i: cols(X1[(m - 2) % 4], i), WS0[p], MV0[p], RS0[p], G4, a_rs0, k - 1, a_x1)
                if has(4):
                    p = m % 2
                    apply(lambda i: x2[:, bass.ds(((k - 4) * G4 + i) * D, D)], WS1[p], MV1[p], RS1[p], G4,
                          a_rs1, k - 3, a_x2)
                if has(1):
                    p = (m - 1) % 2
                    dve.wait_ge(a_z0, k)
                    nc.vector.tensor_tensor(v4(U[:, :]), v4(bank[2][:, :]), bc4(bias0_bc), ALU.add)\
                      .then_inc(a_u, 1)
                    dve.wait_ge(a_u, k)
                    nc.vector.tensor_scalar(V[:, :], U[:, :], 0.0, alpha[:, 0:1], ALU.min, ALU.mult)\
                      .then_inc(a_m, 1)
                    dve.wait_ge(a_m, k)
                    nc.vector.scalar_tensor_tensor(V[:, :], U[:, :], 0.0, V[:, :], ALU.max, ALU.add)\
                      .then_inc(a_v, 1)
                    dve.wait_ge(a_v, k)
                    nc.vector.tensor_tensor(WS0[p][:, :], V[:, :], X0[(m - 1) % 4][:, :], ALU.add)\
                      .then_inc(a_w0, 1)
                    norm(WS0[p], ST0, MV0[p], G4, a_w0, k, a_bs0, a_mv0)
                if has(3):
                    p = (m - 3) % 2
                    dve.wait_ge(a_z1, k - 2)
                    dve.wait_ge(a_x1b, k - 2)
                    nc.vector.tensor_tensor(WS1[p][:, :], bank[4][:, :], X1B[p][:, :], ALU.add)\
                      .then_inc(a_w1, 1)
                    norm(WS1[p], ST1, MV1[p], G4, a_w1, k - 2, a_bs1, a_mv1)
            run_a(dve, step_a)

            def half_b(first, second, tails, after):
                if second:
                    s, l, it = second
                    n1 = it * L + l + 1
                    dve.wait_ge(b_r[s], n1)
                    nc.vector.scalar_tensor_tensor(RT[s][:, :], bank[4 * s + 2][:, :], bhh[:, 2:3],
                                                   RT[s][:, :], ALU.add, ALU.mult).then_inc(b_t1[s], 1)
                if second:
                    s, l, it = second
                    n1 = it * L + l + 1
                    dve.wait_ge(b_t1[s], n1)
                    dve.wait_ge(b_I[s], n1)
                    nc.vector.tensor_tensor(RT[s][:, :], bank[4 * s + 3][:, :], RT[s][:, :], ALU.add)\
                      .then_inc(b_t2[s], 1)
                if first:
                    s, l, it = first
                    n1 = it * L + l + 1
                    if l == 0:
                        dve.wait_ge(b_hth[s], n1)
                        nc.vector.tensor_copy(HT[s][:, :], bank[4 * s + 2][:, :]).then_inc(b_h0[s], 1)
                        dve.wait_ge(b_lda[s], 16 * it + 16)
                        nc.vector.tensor_scalar(A16[s][:, :], ADJR[s][:, :], 0.0, None, ALU.not_equal)\
                          .then_inc(b_a16[s], 1)
                        dve.wait_ge(b_hnh[s], n1)
                        nc.vector.tensor_tensor(HN_LO[s][:, :], X2S[s][:, :], HN_HI[s][:, :], ALU.subtract)\
                          .then_inc(b_hnl[s], 1)
                    else:
                        dve.wait_ge(b_hnh[s], n1)
                        nc.vector.tensor_tensor(HN_LO[s][:, :], bank[4 * s + 3][:, :], HN_HI[s][:, :],
                                                ALU.subtract).then_inc(b_hnl[s], 1)
                if tails[1]:
                    s, l, it = tails[1]
                    norm(YB[s], STB[s], MVB[s], G4, b_y[s], it + 1, b_bs[s], b_mv[s])
                if tails[2]:
                    s, l, it = tails[2]
                    q = it * 2 + s
                    apply(lambda i: x2[:, bass.ds((q * G4 + i) * D, D)], YB[s], MVB[s], RSB[s], G4,
                          b_rs[s], it + 1, b_x3[s])
                if second:
                    s, l, it = second
                    n1 = it * L + l + 1
                    dve.wait_ge(b_n[s], n1)
                    dve.wait_ge(b_w[s], n1)
                    nc.vector.tensor_tensor(RT[s][:, :], RT[s][:, :], WB[s][:, :], ALU.mult)\
                      .then_inc(b_q[s], 1)
                if first:
                    s, l, it = first
                    n1 = it * L + l + 1
                    dve.wait_ge(b_ph[s], n1)
                    nc.vector.tensor_tensor(PT_LO[s][:, :], bank[4 * s + 3][:, :],
                                            PT_HI[s][:, :].bitcast(F32), ALU.subtract).then_inc(b_pl[s], 1)
                if second:
                    s, l, it = second
                    n1 = it * L + l + 1
                    dve.wait_ge(b_q[s], n1)
                    dve.wait_ge(b_zh[s], n1)
                    nc.vector.tensor_tensor(HT[s][:, :], RT[s][:, :], ZH[s][:, :], ALU.add)\
                      .then_inc(b_h[s], 1)
            run_b(dve, half_b)

            def step_c(k, m, has):
                if has(2):
                    dve.wait_ge(c_f, k - 1)
                    xs = x2[0:NODES, bass.ds((k - 2) * G8 * D, G8 * D)]
                    nc.vector.tensor_tensor(xs, bank67[0:NODES, :], xs, ALU.add).then_inc(c_x, 1)
                    wait_apart(dve, c_x, k - 1)
                    for i in range(G8):
                        last = nc.vector.bn_stats(STC[:, 6 * i:6 * i + 6],
                                                  x2[:, bass.ds(((k - 2) * G8 + i) * D, D)])
                    last.then_inc(c_bs, 1)
                    wait_apart(dve, c_bs, k - 1)
                    for i in range(G8):
                        last = nc.vector.bn_aggr(MVC[:, (m * G8 + i) * 2:(m * G8 + i) * 2 + 2],
                                                 STC[:, 6 * i:6 * i + 6])
                    last.then_inc(c_mv, 1)
                if has(0):
                    dve.wait_ge(c_h[1], k + 1)
                    for g in range(NG):
                        v = HID[1][:, :].rearrange("p (s c) -> p s c", c=SLOTS)
                        pv = bank[2][:, 0:SL8].rearrange("p (s c) -> p s c", c=SLOTS)
                        nc.vector.tensor_scalar(v[:, :, OFFS[g]:OFFS[g] + SIZES[g]],
                                                pv[:, :, OFFS[g]:OFFS[g] + SIZES[g]],
                                                b1T[:, g * HC + 1:g * HC + 2], 0.0, ALU.add, ALU.max)\
                          .then_inc(c_rh[1], 1)
                if has(2):
                    dve.wait_ge(c_rs, k - 1)
                    if has(4):
                        dve.wait_ge(c_out[m], (k - m) * 8 - 16)
                    for i in range(G8):
                        c = m * G8 + i
                        last = nc.vector.tensor_scalar(YO[:, c * D:(c + 1) * D],
                                                       x2[:, bass.ds(((k - 2) * G8 + i) * D, D)],
                                                       MVC[:, 2 * c:2 * c + 1], RSC[:, c:c + 1],
                                                       ALU.subtract, ALU.mult)
                    last.then_inc(c_yo, 1)
                if has(1):
                    ov = OT[:, :].rearrange("p (s c) -> p s c", c=SLOTS)
                    dve.wait_ge(c_ro, NG * k)
                    done = 0
                    for g in range(1, NG):
                        at = OFFS[g]
                        for n0, cnt in RUNS[g]:
                            if done:
                                dve.wait_ge(c_add, (k - 1) * ADDS + done)
                            nc.vector.tensor_tensor(ov[:, :, n0:n0 + cnt], ov[:, :, n0:n0 + cnt],
                                                    ov[:, :, at:at + cnt], ALU.add).then_inc(c_add, 1)
                            at += cnt
                            done += 1
            run_c(dve, step_c)

        @block.tensor
        def _(pe):
            mm = nc.tensor.matmul

            pe.wait_ge(w_ident, 2)
            pe.wait_ge(w_ld_tr, 16 * 8)
            nc.tensor.transpose(bank[5][:, 0:P], mask_sb[:, :], ident[:, :])
            nc.tensor.transpose(bank[5][:, 2 * P:2 * P + SMALL], small[:, :], ident[0:SMALL, 0:SMALL])
            for g in range(3):
                nc.tensor.transpose(bank[6][:, g * P:(g + 1) * P], cols(sc_raw, g), ident[:, :])
                nc.tensor.transpose(bank[7][:, g * P:(g + 1) * P], cols(sc_raw, 3 + g), ident[:, :])
            for l in range(L):
                dst = bank[4][:, l * P:(l + 1) * P] if l < 4 else bank[5][:, P:2 * P]
                last = nc.tensor.transpose(dst, cols(sc_raw, 6 + l), ident[:, :])
            last.then_inc(w_tr, 1)
            pe.wait_ge(w_ev, 5)
            for l in range(L):
                mm(bank[l][:, 0:GATE], cols(wT, 3 + l), wT[:, 0:GATE], start=True, stop=True)\
                    .then_inc(w_prod, 1)
            pe.wait_ge(w_lo, L + 1)
            pe.wait_ge(w_ld_misc, 16 * 7)

            def four(dst, lhs, rhs, signal):
                for i in range(G4):
                    last = mm(cols(dst, i), lhs(i), rhs(i), start=True, stop=True)
                last.then_inc(signal, 1)

            def step_a(k, m, has):
                if has(0):
                    pe.wait_ge(a_ld[m], (k - m) * 8 + 32)
                    if has(1):
                        pe.wait_ge(a_adjT, k)
                    for i in range(G4):
                        last = nc.tensor.transpose(cols(bank[0], i), cols(ADJ[m], i), ident[:, :])
                    last.then_inc(a_tadj, 1)
                if has(2):
                    pe.wait_ge(a_x1, k - 1)
                    mp = (m - 2) % 4
                    four(bank[3], lambda i: cols(X1[mp], i), lambda i: cols(ADJT[mp], i), a_y1)
                if has(0):
                    pe.wait_ge(a_adjT, k + 1)
                    four(bank[1], lambda i: cols(X0[m], i), lambda i: cols(ADJT[m], i), a_y0)
                if has(2):
                    pe.wait_ge(a_yT1, k - 1)
                    if has(3):
                        pe.wait_ge(a_w1, k - 2)
                    four(bank[4], lambda i: cols(YT1, i), lambda i: w1_sb[:, :], a_z1)
                if has(0):
                    pe.wait_ge(a_yT0, k + 1)
                    if has(1):
                        pe.wait_ge(a_u, k)
                    four(bank[2], lambda i: cols(YT0, i), lambda i: w0_sb[:, :], a_z0)
            run_a(pe, step_a)

            def hi_passes(dst, w_h, w_l, col, h, start):
                mm(dst[:, :], w_h[:, col:col + P], h[:, :], start=start, stop=False)
                mm(dst[:, :], w_l[:, col:col + P], h[:, :], start=False, stop=False)

            def lo_pass(dst, w_h, col, lo, stop):
                return mm(dst[:, :], w_h[:, col:col + P], lo[:, :], start=False, stop=stop)

            def start(s, it):
                pe.wait_ge(b_ldx[s], 16 * it + 16)
                if not (isinstance(it, int) and it == 0):
                    pe.wait_ge(b_t1[s], it * L)
                for i in range(G4):
                    last = nc.tensor.transpose(cols(bank[4 * s + 2], i), cols(X2S[s], i), ident[:, :])
                last.then_inc(b_t0[s], 1)

            def half_b(first, second, tails, after):
                if first and not second:
                    start(first[0], first[2])
                if second:
                    s, l, it = second
                    g = l * GATE
                    hi_passes(bank[4 * s + 3], wx_hi, wx_lo, g + 2 * P, PT_HI[s], True)
                    lo_pass(bank[4 * s + 3], wx_hi, g + 2 * P, PT_LO[s], True).then_inc(b_I[s], 1)
                    lo_pass(bank[4 * s + 1], wx_hi, g + P, PT_LO[s], True).then_inc(b_Z[s], 1)
                if first:
                    s, l, it = first
                    n1 = it * L + l + 1
                    pe.wait_ge(b_hth[s], n1)
                    if l == 0:
                        pe.wait_ge(b_h0[s], it + 1)
                    for b in range(3):
                        hi_passes(bank[4 * s + b], wh_hi, wh_lo, b * P, HT_HI[s], True)
                    if l == 0:
                        pe.wait_ge(b_a16[s], it + 1)
                    pe.wait_ge(b_hnl[s], n1)
                    if l == 0 and not (isinstance(it, int) and it == 0):
                        pe.wait_ge(b_ye[s], it)
                    for i in range(G4):
                        mm(cols(bank[4 * s + 3], i), cols(HN_HI[s], i), cols(A16[s], i), start=True, stop=False)
                        last = mm(cols(bank[4 * s + 3], i), cols(HN_LO[s], i), cols(A16[s], i),
                                  start=False, stop=True)
                    last.then_inc(b_at[s], 1)
                    pe.wait_ge(b_htl[s], n1)
                    for b in range(3):
                        lo_pass(bank[4 * s + b], wh_hi, b * P, HT_LO[s], b == 2)
                    pe.wait_ge(b_ph[s], n1)
                    for b in range(2):
                        hi_passes(bank[4 * s + b], wx_hi, wx_lo, l * GATE + b * P, PT_HI[s], False)
                    pe.wait_ge(b_pl[s], n1)
                    lo_pass(bank[4 * s + 0], wx_hi, l * GATE, PT_LO[s], True).then_inc(b_R[s], 1)
                if after:
                    start(after[0], after[2])
                if second:
                    s, l, it = second
                    n1 = it * L + l + 1
                    pe.wait_ge(b_h[s], n1)
                    for i in range(G4):
                        last = nc.tensor.transpose(cols(bank[4 * s + 3], i), cols(HT[s], i), ident[:, :])
                    last.then_inc(b_tp[s], 1)
            pe.wait_ge(a_x2, STEPS_A)
            run_b(pe, half_b)

            def sl(t, g):
                return t.rearrange("p (s c) -> p s c", c=SLOTS)[:, :, OFFS[g]:OFFS[g] + SIZES[g]]

            W2 = 2 * SLOTS

            def step_c(k, m, has):
                if has(2):
                    pe.wait_ge(c_add, (k - 1) * ADDS)
                    if has(3):
                        pe.wait_ge(c_x, k - 2)
                    for i in range(G8):
                        last = nc.tensor.transpose(bank67[0:NODES, i * P:(i + 1) * P],
                                                   OT[:, i * SLOTS:i * SLOTS + NODES], ident[:, :])
                    last.then_inc(c_f, 1)
                if has(1):
                    pe.wait_ge(c_tt, k)
                    for i in range(G8 // 2):
                        last = nc.tensor.transpose(bank[4][0:W2, i * P:(i + 1) * P],
                                                   TT[:, i * W2:(i + 1) * W2], ident[:, :])
                    last.then_inc(c_n, 1)
                if has(0):
                    pe.wait_ge(c_ldx, 16 * k + 16)
                    for i in range(G8):
                        last = mm(bank[0][:, i * SLOTS:(i + 1) * SLOTS], X3S[0:NODES, i * D:(i + 1) * D],
                                  mt[0:NODES, bass.ds((k * G8 + i) * SLOTS, SLOTS)], start=True, stop=True)
                    last.then_inc(c_s, 1)
                if has(1):
                    pe.wait_ge(c_tn, k)
                    for i in range(G8 // 2):
                        last = mm(bank[5][:, i * W2:(i + 1) * W2], TN[0:W2, i * P:(i + 1) * P],
                                  n2[0:W2, bass.ds(((k - 1) * (G8 // 2) + i) * W2, W2)], start=True, stop=True)
                    last.then_inc(c_o, 1)
                if has(0):
                    pe.wait_ge(c_st, k + 1)
                    for c in range(HC):
                        for g in range(NG):
                            last = mm(sl(bank[1 + c][:, 0:SL8], g), v1[:, (g * HC + c) * P:(g * HC + c + 1) * P],
                                      sl(SP_T[:, :], g), start=True, stop=True)
                        last.then_inc(c_h[c], 1)
                    for g in range(NG):
                        for c in range(HC):
                            pe.wait_ge(c_rh[c], NG * k + g + 1)
                            last = mm(sl(bank[3][:, 0:SL8], g), v2[:, (g * HC + c) * P:(g * HC + c + 1) * P],
                                      sl(HID[c][:, :], g), start=c == 0, stop=c == HC - 1)
                    last.then_inc(c_t, 1)
            pe.wait_ge(l3_ld, 16 * L3_LOADS)
            for s in range(2):
                pe.wait_ge(b_x3[s], ITERS)
            run_c(pe, step_c)


W_BRZ, W_FMX, W_DEG, W_AN, W_ALL = 2, 4, 9, 13, 16
ADDS = sum(len(r) for r in RUNS[1:])
L3_LOADS = sum(len(r) for r in RUNS) + 2 * NG


_INS = ['x', 'adj', 'nodemask', 'L0_gnn_W', 'L0_gnn_bias', 'L0_gnn_prelu_a', 'L1_gnn_weight', 'L1_gnn_bias',
        'L2_gnn_weight', 'L2_gnn_w_ih', 'L2_gnn_w_hh', 'L2_gnn_b_ih', 'L2_gnn_b_hh', 'L3_gnn_W1', 'L3_gnn_b1',
        'L3_gnn_W2', 'L3_gnn_b2', 'L3_gnn_fusion_w']


def kernel(**inputs):
    import numpy as _np
    import concourse.bacc as _bacc
    from concourse import mybir as _mybir
    from concourse.bass_utils import run_bass_kernel_spmd as _run

    nc = _bacc.Bacc("TRN2", target_bir_lowering=False, num_devices=1)
    arrays, args = {}, []
    for name in _INS:
        a = _np.ascontiguousarray(inputs[name])
        if a.ndim == 0:
            a = a.reshape(1)
        arrays[f"in_{name}_dram"] = a
        args.append(nc.dram_tensor(f"in_{name}_dram", a.shape, _mybir.dt.from_np(a.dtype), kind="ExternalInput").ap())
    shape = tuple(inputs['x'].shape)
    args.append(nc.dram_tensor("out_0_dram", shape, _mybir.dt.float32, kind="ExternalOutput").ap())
    graph_stack_kernel(nc, *args)
    r = _run(nc, [arrays], core_ids=[0])
    return r.results[0]["out_0_dram"]
```

```python
from contextlib import ExitStack

import concourse.bass as bass
from concourse import mybir

ALU = mybir.AluOpType
ACT = mybir.ActivationFunctionType
F32 = mybir.dt.float32
F32R = mybir.dt.float32r
F16 = mybir.dt.float16
AX_X = mybir.AxisListType.X

P = 128
EPS = 1e-5

RUNS = [[(0, 25)], [(0, 9)], [(0, 1), (9, 6)], [(6, 3), (12, 3)], [(3, 3), (9, 3)]]
SIZES = [sum(n for _, n in runs) for runs in RUNS]
OFFS = [sum(SIZES[:g]) for g in range(len(SIZES))]
SLOTS = sum(SIZES)
NODES = SIZES[0]
NG = len(RUNS)
SQ = [n * n for n in SIZES]
SQ_OFFS = [sum(SQ[:g]) for g in range(NG)]


def graph_stack_kernel(nc, x, adj, nodemask, w0, bias0, prelu_a, w1, bias1, gw, w_ih, w_hh,
                       b_ih, b_hh, l3_w1, l3_b1, l3_w2, l3_b2, fusion_w, out):
    B, N, D = x.shape
    L = gw.shape[0]
    G4 = 4
    STEPS_A = B // G4
    ITERS = B // (2 * G4)
    GC = 16
    STEPS_C = B // GC
    PAIRS = GC // 2
    ON_POOL = 8
    ON_ACT = GC - ON_POOL
    GATE = 3 * D
    HC = l3_w1.shape[2] // P
    CS = GC * SLOTS
    SMALL = 6 + NG + NG * HC
    assert N == P and D == P

    an_dram = nc.dram_tensor("an_dram", (B, sum(SQ)), F32, kind="Internal").ap()
    adj_nm = adj.rearrange("s n m -> n s m")
    x_nm = x.rearrange("s n d -> n s d")
    out_nm = out.rearrange("s n d -> n s d")

    ctx = ExitStack()
    with ctx:
        def sem(name):
            return ctx.enter_context(nc.semaphore(name))

        def sb(name, shape, dt=F32, scope=ctx):
            return scope.enter_context(nc.sbuf_tensor(name, shape, dt))

        x2 = sb("x2", [P, B * D])
        ident = sb("ident", [P, P])
        w0_sb = sb("w0_sb", [P, D])
        w1_sb = sb("w1_sb", [P, D])
        bias0_bc = sb("bias0_bc", [P, D])
        bias1_bc = sb("bias1_bc", [P, D])
        alpha = sb("alpha", [P, 1])
        smallT = sb("smallT", [P, SMALL])
        bih, bhh = smallT[:, 0:3], smallT[:, 3:6]
        b2T, b1T = smallT[:, 6:6 + NG], smallT[:, 6 + NG:SMALL]
        nbz = sb("nbz", [P, 1])
        brz = sb("brz", [P, 2])
        maskT = sb("maskT", [P, B])
        half = sb("half", [P, GC])
        eps = sb("eps", [P, GC])
        wx_hi = sb("wx_hi", [P, L * GATE], F32R)
        wx_lo = sb("wx_lo", [P, L * GATE], F32R)
        wh_hi = sb("wh_hi", [P, GATE], F32R)
        wh_lo = sb("wh_lo", [P, GATE], F32R)
        v1 = sb("v1", [P, NG * HC * P])
        v2 = sb("v2", [P, NG * HC * P])
        nw = sb("nw", [P, NG])
        nwb2 = sb("nwb2", [P, NG])
        anT = sb("anT", [P, sum(SQ)])

        psum = ctx.enter_context(nc.psum_tensor("psum", [P, 8 * 512], F32))
        bank = [psum[:, i * 512:(i + 1) * 512] for i in range(8)]

        sa = ExitStack()
        sc_raw = sb("wraw", [P, (2 * 3 + L) * P], scope=sa)
        wT = sb("wT", [P, (3 + L) * P], scope=sa)
        mask_sb = sb("mask_sb", [P, P], scope=sa)
        small = sb("small", [SMALL, P], scope=sa)
        fw = sb("fw", [P, NG], scope=sa)
        fmx = sb("fmx", [P, 1], scope=sa)
        fsum = sb("fsum", [P, 1], scope=sa)
        adj25 = sb("adj25", [P, NODES * NODES], scope=sa)
        cmp_a = sb("cmp_a", [P, sum(SQ)], scope=sa)
        deg = sb("deg", [P, SLOTS], scope=sa)
        deg0 = sb("deg0", [P, SLOTS], scope=sa)
        dinv = sb("dinv", [P, SLOTS], scope=sa)
        half53 = sb("half53", [P, SLOTS], scope=sa)

        ADJ = [sb(f"adj{i}", [P, G4 * N], scope=sa) for i in range(4)]
        X0 = [sb(f"x0_{i}", [P, G4 * D], scope=sa) for i in range(4)]
        ADJT = [sb(f"adjT{i}", [P, G4 * N], scope=sa) for i in range(4)]
        X1 = [sb(f"x1_{i}", [P, G4 * D], scope=sa) for i in range(4)]
        YT0 = sb("yT0", [P, G4 * N], scope=sa)
        YT1 = sb("yT1", [P, G4 * N], scope=sa)
        U = sb("u", [P, G4 * D], scope=sa)
        V = sb("v", [P, G4 * D], scope=sa)
        WS0 = [sb(f"ws0_{i}", [P, G4 * D], scope=sa) for i in range(2)]
        WS1 = [sb(f"ws1_{i}", [P, G4 * D], scope=sa) for i in range(2)]
        X1B = [sb(f"x1b{i}", [P, G4 * D], scope=sa) for i in range(2)]
        ST0, ST1 = (sb(f"st{i}", [P, G4 * 6], scope=sa) for i in range(2))
        MV0 = [sb(f"mv0_{i}", [P, G4 * 2], scope=sa) for i in range(2)]
        MV1 = [sb(f"mv1_{i}", [P, G4 * 2], scope=sa) for i in range(2)]
        NM1 = [sb(f"nm1_{i}", [P, G4], scope=sa) for i in range(2)]
        VE0, VE1 = (sb(f"ve{i}", [P, G4], scope=sa) for i in range(2))
        RS0 = [sb(f"rs0_{i}", [P, G4], scope=sa) for i in range(2)]
        RS1 = [sb(f"rs1_{i}", [P, G4], scope=sa) for i in range(2)]
        sa.close()

        m2 = sb("m2", [P, B // 2 * 2 * SLOTS])
        n2 = sb("n2", [P, B // 2 * 2 * SLOTS])
        sbb = ExitStack()
        ADJR = [sb(f"adjr{s}", [P, G4 * N], scope=sbb) for s in range(2)]
        A16 = [sb(f"a16_{s}", [P, G4 * N], F16, scope=sbb) for s in range(2)]
        X2S = [sb(f"x2s{s}", [P, G4 * D], scope=sbb) for s in range(2)]
        HT = [sb(f"ht{s}", [P, G4 * N], scope=sbb) for s in range(2)]
        HT_HI = [sb(f"hth{s}", [P, G4 * N], F32R, scope=sbb) for s in range(2)]
        HT_LO = [sb(f"htl{s}", [P, G4 * N], F32R, scope=sbb) for s in range(2)]
        PT_HI = [sb(f"pth{s}", [P, G4 * N], F32R, scope=sbb) for s in range(2)]
        PT_LO = [sb(f"ptl{s}", [P, G4 * N], F32R, scope=sbb) for s in range(2)]
        HN_HI = [sb(f"hnh{s}", [P, G4 * D], F16, scope=sbb) for s in range(2)]
        HN_LO = [sb(f"hnl{s}", [P, G4 * D], F16, scope=sbb) for s in range(2)]
        RT = [sb(f"rt{s}", [P, G4 * N], scope=sbb) for s in range(2)]
        ZW = [sb(f"zw{s}", [P, G4 * N], scope=sbb) for s in range(2)]
        ZH = [sb(f"zh{s}", [P, G4 * N], scope=sbb) for s in range(2)]
        WB = [sb(f"wb{s}", [P, G4 * N], scope=sbb) for s in range(2)]
        YB = [sb(f"yb{s}", [P, G4 * D], scope=sbb) for s in range(2)]
        STB = [sb(f"stb{s}", [P, G4 * 6], scope=sbb) for s in range(2)]
        MVB = [sb(f"mvb{s}", [P, G4 * 2], scope=sbb) for s in range(2)]
        VEB = [sb(f"veb{s}", [P, G4], scope=sbb) for s in range(2)]
        RSB = [sb(f"rsb{s}", [P, G4], scope=sbb) for s in range(2)]
        sbb.close()

        X3S = sb("x3s", [P, PAIRS * D])
        SP_T = sb("sp_t", [P, CS])
        HID = [sb(f"hid{c}", [P, CS]) for c in range(HC)]
        TT = sb("tt", [P, CS])
        TN = sb("tn", [P, PAIRS * P])
        OT = sb("ot", [P, CS])
        YO = sb("yo", [P, 2 * GC * D])
        STC = sb("stc", [P, GC * 6])
        MVC = sb("mvc", [P, 2 * GC * 2])
        VEC = sb("vec", [P, GC])
        RSC = sb("rsc", [P, 2 * GC])
        NMC = sb("nmc", [P, 2 * GC])

        w_ld_tr = sem("w_ld_tr")
        w_ld_a25 = sem("w_ld_a25")
        w_ld_fw = sem("w_ld_fw")
        w_ld_misc = sem("w_ld_misc")
        w_ident = sem("w_ident")
        w_consts = sem("w_consts")
        w_tr = sem("w_tr")
        w_ev = sem("w_ev")
        w_prod = sem("w_prod")
        w_hi = sem("w_hi")
        w_lo = sem("w_lo")
        w_v = sem("w_v")
        w_exp = sem("w_exp")
        w_pow = sem("w_pow")
        an_st = sem("an_st")
        n2_zero = sem("n2_zero")
        l3_ld = sem("l3_ld")

        a_ld = [sem(f"a_ld{i}") for i in range(4)]
        a_tadj = sem("a_tadj")
        a_adjT = sem("a_adjT")
        a_y0, a_yT0, a_z0 = sem("a_y0"), sem("a_yT0"), sem("a_z0")
        a_y1, a_yT1, a_z1 = sem("a_y1"), sem("a_yT1"), sem("a_z1")
        a_u, a_m, a_v, a_w0 = sem("a_u"), sem("a_m"), sem("a_v"), sem("a_w0")
        a_w1 = sem("a_w1")
        a_bs0, a_mv0, a_ve0, a_rs0 = sem("a_bs0"), sem("a_mv0"), sem("a_ve0"), sem("a_rs0")
        a_bs1, a_mv1, a_ve1, a_rs1 = sem("a_bs1"), sem("a_mv1"), sem("a_ve1"), sem("a_rs1")
        a_nm1 = sem("a_nm1")
        a_x1, a_x1b, a_x2 = sem("a_x1"), sem("a_x1b"), sem("a_x2")

        def sem2(name):
            return [sem(f"{name}{s}") for s in range(2)]

        b_ldx, b_lda, b_a16 = sem2("b_ldx"), sem2("b_lda"), sem2("b_a16")
        b_t0, b_h0 = sem2("b_t0"), sem2("b_h0")
        b_hnh, b_hnl, b_hth, b_htl = sem2("b_hnh"), sem2("b_hnl"), sem2("b_hth"), sem2("b_htl")
        b_at, b_ph, b_pl = sem2("b_at"), sem2("b_ph"), sem2("b_pl")
        b_R, b_I, b_Z = sem2("b_R"), sem2("b_I"), sem2("b_Z")
        b_r, b_t1, b_t2, b_z, b_n = sem2("b_r"), sem2("b_t1"), sem2("b_t2"), sem2("b_z"), sem2("b_n")
        b_zh, b_w, b_q, b_h, b_tp = sem2("b_zh"), sem2("b_w"), sem2("b_q"), sem2("b_h"), sem2("b_tp")
        b_ye, b_ym = sem2("b_ye"), sem2("b_ym")
        b_y, b_bs, b_mv, b_ve, b_rs, b_x3 = (sem2("b_y"), sem2("b_bs"), sem2("b_mv"), sem2("b_ve"),
                                             sem2("b_rs"), sem2("b_x3"))

        c_ldx, c_s, c_st = sem("c_ldx"), sem("c_s"), sem("c_st")
        c_h = [sem(f"c_h{c}") for c in range(HC)]
        c_rh = [sem(f"c_rh{c}") for c in range(HC)]
        c_t, c_tt, c_tts, c_n, c_tn = sem("c_t"), sem("c_tt"), sem("c_tts"), sem("c_n"), sem("c_tn")
        c_nm = sem("c_nm")
        c_yoh = sem("c_yoh")
        c_dev = sem("c_dev")
        c_yop = sem("c_yop")
        c_o, c_ro, c_add, c_f = sem("c_o"), sem("c_ro"), sem("c_add"), sem("c_f")
        c_x, c_bs, c_mv, c_ve, c_rs = sem("c_x"), sem("c_bs"), sem("c_mv"), sem("c_ve"), sem("c_rs")
        c_out = [sem(f"c_out{i}") for i in range(2)]

        block = ctx.enter_context(nc.Block())

        def steps_a(role):
            last_lag = 4
            total = STEPS_A + last_lag

            def peeled(k):
                role(k, k % 4, lambda lag: 0 <= k - lag < STEPS_A)
            return peeled, total

        def run_a(eng, role):
            peeled, total = steps_a(role)
            for k in range(4):
                peeled(k)
            with eng.Fori(1, STEPS_A // 4) as j:
                for m in range(4):
                    role(j * 4 + m, m, lambda lag: True)
            for k in range(STEPS_A, total):
                peeled(k)

        items = [(s, l) for l in range(L) for s in range(2)]

        def run_b(eng, half_step):
            def item(i, it):
                n = len(items)
                at = it + i // n
                if isinstance(at, int) and not 0 <= at < ITERS:
                    return None
                return (*items[i % n], at)

            def half(j, it):
                second = item(j, it)
                tails = [t if t and t[1] == L - 1 else None for t in (item(j - 1, it), item(j - 3, it), item(j - 5, it))]
                after = item(j + 2, it) if second and second[1] == L - 1 else None
                half_step(item(j + 1, it), second, tails, after)

            def body(it):
                for j in range(len(items)):
                    half(j, it)
            half_step(item(0, 0), None, [None] * 3, item(1, 0))
            body(0)
            with eng.Fori(1, ITERS - 1) as it:
                body(it)
            body(ITERS - 1)
            for j in range(5):
                half(len(items) + j, ITERS - 1)

        def run_c(eng, step):
            for k in range(4):
                step(k, k % 2, lambda lag: k - lag >= 0)
            with eng.Fori(2, STEPS_C // 2) as j:
                for m in range(2):
                    step(j * 2 + m, m, lambda lag: True)
            for k in range(STEPS_C, STEPS_C + 3):
                step(k, k % 2, lambda lag: k - lag < STEPS_C)

        def wait_apart(eng, signal, value):
            eng.wait_ge(w_ident, 2)
            eng.wait_ge(signal, value)

        def slots(t, g):
            return t.rearrange("p (s c) -> p s c", c=SLOTS)[:, :, OFFS[g]:OFFS[g] + SIZES[g]]

        def slots2(lo, g):
            two = psum[:, lo * 512:(lo + 2) * 512].rearrange("p (b x) -> p b x", b=2)[:, :, 0:GC // 2 * SLOTS]
            return two.rearrange("p b (s c) -> p b s c", c=SLOTS)[:, :, :, OFFS[g]:OFFS[g] + SIZES[g]]

        def by_group(lo, g):
            c = GC * (OFFS[g] - NODES) if g else 0
            return bank[lo + (g > 0)][:, c:c + GC * SIZES[g]]

        def grp(t, g):
            return t[:, GC * OFFS[g]:GC * (OFFS[g] + SIZES[g])]

        def per_graph(ap, g):
            return ap.rearrange("p (s n) -> p s n", n=SIZES[g])

        def cols(t, i):
            return t[:, i * P:(i + 1) * P]

        def bc4(t):
            return t[:, :].unsqueeze(1).to_broadcast([P, G4, D])

        def v4(t):
            return t.rearrange("p (s d) -> p s d", s=G4)

        @block.sync
        def _(sp):
            sp.dma_start(sc_raw[:, 0:3 * P].rearrange("p (g d) -> p g d", g=3),
                         w_ih.rearrange("(g p) d -> p g d", p=P)).then_inc(w_ld_tr, 16)
            sp.dma_start(sc_raw[:, 3 * P:6 * P].rearrange("p (g d) -> p g d", g=3),
                         w_hh.rearrange("(g p) d -> p g d", p=P)).then_inc(w_ld_tr, 16)
            sp.dma_start(sc_raw[:, 6 * P:(6 + L) * P].rearrange("p (g d) -> p g d", g=L),
                         gw.rearrange("l p d -> p l d")).then_inc(w_ld_tr, 16)
            sp.dma_start(mask_sb[:, :], nodemask).then_inc(w_ld_tr, 16)
            sp.dma_start(small[0:3, :], b_ih.rearrange("(g p) -> g p", p=P)).then_inc(w_ld_tr, 16)
            sp.dma_start(small[3:6, :], b_hh.rearrange("(g p) -> g p", p=P)).then_inc(w_ld_tr, 16)
            sp.dma_start(small[6:6 + NG, :], l3_b2).then_inc(w_ld_tr, 16)
            sp.dma_start(small[6 + NG:SMALL, :], l3_b1.rearrange("g (c p) -> (g c) p", p=P)).then_inc(w_ld_tr, 16)
            sp.dma_start(w0_sb[:, :], w0).then_inc(w_ld_misc, 16)
            sp.dma_start(w1_sb[:, :], w1).then_inc(w_ld_misc, 16)
            sp.dma_start(bias0_bc[:, :], bias0.partition_broadcast(P)).then_inc(w_ld_misc, 16)
            sp.dma_start(bias1_bc[:, :], bias1.partition_broadcast(P)).then_inc(w_ld_misc, 16)
            sp.dma_start(alpha[:, :], prelu_a.partition_broadcast(P)).then_inc(w_ld_misc, 16)

            def load_a(k, m, has):
                if not has(0):
                    return
                if not (isinstance(k, int) and k < 4):
                    sp.wait_ge(a_w0, k - 3)
                sp.dma_start(v4(ADJ[m][:, :]), adj_nm[:, bass.ds(k * G4, G4), :]).then_inc(a_ld[m], 16)
                sp.dma_start(v4(X0[m][:, :]), x_nm[:, bass.ds(k * G4, G4), :]).then_inc(a_ld[m], 16)
            for k in range(4):
                load_a(k, k, lambda lag: True)
            sp.dma_start(adj25[:, :].rearrange("s (i j) -> s i j", i=NODES),
                         adj[:, 0:NODES, 0:NODES]).then_inc(w_ld_a25, 16)
            sp.dma_start(fw[:, :], fusion_w.partition_broadcast(P)).then_inc(w_ld_fw, 16)
            sp.dma_start(v1[:, :].rearrange("p (g e) -> p g e", g=NG),
                         l3_w1.rearrange("g p e -> p g e")).then_inc(w_ld_misc, 16)
            sp.dma_start(v2[:, :].rearrange("p (g c d) -> p g c d", g=NG, c=HC),
                         l3_w2.rearrange("g (c p) d -> p g c d", p=P)).then_inc(w_ld_misc, 16)
            with sp.Fori(1, STEPS_A // 4) as j:
                for m in range(4):
                    load_a(j * 4 + m, m, lambda lag: True)

            def load_b(s, it):
                if not (isinstance(it, int) and it == 0):
                    sp.wait_ge(b_t0[s], it)
                    sp.wait_ge(b_hnl[s], L * it - (L - 1))
                    sp.wait_ge(b_a16[s], it)
                q = it * 2 + s
                sp.dma_start(X2S[s][:, :], x2[:, bass.ds(q * G4 * D, G4 * D)]).then_inc(b_ldx[s], 16)
                sp.dma_start(v4(ADJR[s][:, :]), adj_nm[:, bass.ds(q * G4, G4), :]).then_inc(b_lda[s], 16)
            sp.wait_ge(w_v, W_AN)
            sp.dma_start(an_dram, anT[:, :]).then_inc(an_st, 16)
            sp.wait_ge(a_x2, STEPS_A)
            for s in range(2):
                load_b(s, 0)
            sp.wait_ge(n2_zero, 4)
            sp.wait_ge(an_st, 16)
            n2v = n2[:, :].rearrange("p (q c) -> p q c", c=2 * SLOTS)
            m2v = m2[:, :].rearrange("p (q c) -> p q c", c=2 * SLOTS)
            an = [an_dram[:, SQ_OFFS[g]:SQ_OFFS[g] + SQ[g]].rearrange("s (j i) -> j s i", i=SIZES[g])
                  for g in range(NG)]
            for g in range(NG):
                at = 0
                for m0, cnt in RUNS[g]:
                    for par in range(2):
                        r, c = par * NODES + m0, par * SLOTS + OFFS[g]
                        sp.dma_start(m2v[r:r + cnt, :, c:c + SIZES[g]], an[g][at:at + cnt, par:B:2, :])\
                          .then_inc(l3_ld, 16)
                    at += cnt
                for par in range(2):
                    r = par * SLOTS + OFFS[g]
                    sp.dma_start(n2v[r:r + SIZES[g], :, r:r + SIZES[g]], an[g][:, par:B:2, :])\
                      .then_inc(l3_ld, 16)
            with sp.Fori(1, ITERS) as it:
                for s in range(2):
                    load_b(s, it)

            def step_c(k, m, has):
                if has(0):
                    if isinstance(k, int) and k == 0:
                        for s in range(2):
                            sp.wait_ge(b_x3[s], ITERS * G4)
                    else:
                        sp.wait_ge(c_s, k)
                    xv = x2[0:NODES, bass.ds(k * GC * D, GC * D)].rearrange("p (i t d) -> p i t d", t=2, d=D)
                    for par in range(2):
                        sp.dma_start(X3S[par * NODES:(par + 1) * NODES, :].rearrange("p (i d) -> p i d", d=D),
                                     xv[:, :, par, :]).then_inc(c_ldx, 16)
                if has(3):
                    sp.wait_ge(c_yoh, 2 * (k - 2))
                    sp.wait_ge(c_yop, k - 2)
                    h = (m + 1) % 2
                    sp.dma_start(out_nm[:, bass.ds((k - 3) * GC, GC), :],
                                 YO[:, h * GC * D:(h + 1) * GC * D].rearrange("p (s d) -> p s d", s=GC))\
                      .then_inc(c_out[h], 16)
            run_c(sp, step_c)
            for i in range(2):
                sp.wait_ge(c_out[i], 16 * (STEPS_C // 2))

        @block.gpsimd
        def _(pool):
            nc.gpsimd.memset(ident[:, :], 0.0).then_inc(w_ident, 1)
            pool.wait_ge(w_ident, 1)
            nc.gpsimd.affine_select(out=ident[:, :], in_=ident[:, :], compare_op=ALU.not_equal, fill=1.0,
                                    base=0, pattern=[[-1, P]], channel_multiplier=1).then_inc(w_ident, 1)
            nc.gpsimd.memset(half[:, :], -0.5).then_inc(w_consts, 1)
            nc.gpsimd.memset(half53[:, :], -0.5).then_inc(w_consts, 1)
            nc.gpsimd.memset(eps[:, :], EPS).then_inc(w_consts, 1)
            pool.wait_ge(w_consts, 3)
            pool.wait_ge(w_v, W_DEG)
            nc.gpsimd.tensor_tensor(dinv[:, :], deg[:, :], half53[:, :], ALU.pow).then_inc(w_pow, 1)

            def rstd(mv, ve, rs, n, s_mv, at, s_ve, s_rs):
                pool.wait_ge(s_mv, at)
                nc.gpsimd.tensor_tensor(ve[:, :], mv.rearrange("p (s t) -> p s t", t=2)[:, :, 1],
                                        eps[:, 0:n], ALU.add).then_inc(s_ve, 1)
                pool.wait_ge(s_ve, at)
                nc.gpsimd.tensor_tensor(rs, ve[:, :], half[:, 0:n], ALU.pow).then_inc(s_rs, 1)

            def step_a(k, m, has):
                if has(1):
                    pool.wait_ge(a_v, k)
                    nc.gpsimd.tensor_tensor(WS0[(m - 1) % 2][:, :], V[:, :], X0[(m - 1) % 4][:, :], ALU.add)\
                      .then_inc(a_w0, 1)
                if has(2):
                    pool.wait_ge(a_x1, k - 1)
                    nc.gpsimd.tensor_tensor(v4(X1B[m % 2][:, :]), v4(X1[(m - 2) % 4][:, :]),
                                            bc4(bias1_bc), ALU.add).then_inc(a_x1b, 1)
                if has(3):
                    rstd(MV1[(m - 3) % 2][:, :], VE1, RS1[(m - 3) % 2][:, :], G4, a_mv1, k - 2, a_ve1, a_rs1)
                if has(1):
                    rstd(MV0[(m - 1) % 2][:, :], VE0, RS0[(m - 1) % 2][:, :], G4, a_mv0, k, a_ve0, a_rs0)
            pool.wait_ge(w_ld_misc, 16 * 7)
            run_a(pool, step_a)

            pool.wait_ge(a_x2, STEPS_A)
            for h in range(2):
                w = B // 2 * SLOTS
                nc.gpsimd.memset(n2[:, h * w:(h + 1) * w], 0.0).then_inc(n2_zero, 1)
                nc.gpsimd.memset(m2[:, h * w:(h + 1) * w], 0.0).then_inc(n2_zero, 1)

            def half_b(first, second, tails, after):
                if first:
                    s, l, it = first
                    n1 = it * L + l + 1
                    pool.wait_ge(b_hth[s], n1)
                    if l == 0:
                        pool.wait_ge(b_h0[s], it + 1)
                    nc.gpsimd.tensor_tensor(HT_LO[s][:, :], HT[s][:, :], HT_HI[s][:, :].bitcast(F32),
                                            ALU.subtract).then_inc(b_htl[s], 1)
                if second:
                    s, l, it = second
                    n1 = it * L + l + 1
                    pool.wait_ge(b_z[s], n1)
                    nc.gpsimd.tensor_tensor(ZH[s][:, :], ZW[s][:, :], HT[s][:, :], ALU.mult)\
                      .then_inc(b_zh[s], 1)
                if tails[0]:
                    s, l, it = tails[0]
                    q = it * 2 + s
                    wait_apart(pool, b_ye[s], it + 1)
                    nc.gpsimd.tensor_tensor(v4(YB[s][:, :]), v4(YB[s][:, :]),
                                            maskT[:, bass.ds(q * G4, G4)].unsqueeze(2).to_broadcast([P, G4, D]),
                                            ALU.mult).then_inc(b_ym[s], 1)
                    wait_apart(pool, b_ym[s], it + 1)
                    nc.gpsimd.tensor_tensor(YB[s][:, :], YB[s][:, :], x2[:, bass.ds(q * G4 * D, G4 * D)],
                                            ALU.add).then_inc(b_y[s], 1)
                if tails[1]:
                    s, l, it = tails[1]
                    rstd(MVB[s][:, :], VEB[s], RSB[s][:, :], G4, b_mv[s], it + 1, b_ve[s], b_rs[s])
            run_b(pool, half_b)

            def step_c(k, m, has):
                if has(3):
                    wait_apart(pool, c_rs, k - 2)
                    if has(5):
                        wait_apart(pool, c_out[(m + 1) % 2], (k - 3 - (m + 1) % 2) * 8)
                    c0, c1 = (m + 1) % 2 * GC + ON_ACT, (m + 1) % 2 * GC + GC
                    yo = YO[:, c0 * D:c1 * D].rearrange("p (s d) -> p s d", d=D)
                    nc.gpsimd.tensor_tensor(
                        yo, x2[:, bass.ds(((k - 3) * GC + ON_ACT) * D, ON_POOL * D)].rearrange("p (s d) -> p s d", d=D),
                        MVC[:, 2 * c0:2 * c1:2].unsqueeze(2).to_broadcast([P, ON_POOL, D]),
                        ALU.subtract).then_inc(c_dev, 1)
                    pool.wait_ge(c_dev, k - 2)
                    nc.gpsimd.tensor_tensor(yo, yo, RSC[:, c0:c1].unsqueeze(2).to_broadcast([P, ON_POOL, D]),
                                            ALU.mult).then_inc(c_yop, 1)
                if has(2) and has(4):
                    wait_apart(pool, c_yop, k - 3)
                    pool.wait_ge(c_yoh, 2 * (k - 3))
                if has(2):
                    rstd(MVC[:, m * GC * 2:(m + 1) * GC * 2], VEC, RSC[:, m * GC:(m + 1) * GC], GC,
                         c_mv, k - 1, c_ve, c_rs)
            run_c(pool, step_c)

        @block.scalar
        def _(act):
            act.wait_ge(w_tr, 1)
            nc.scalar.activation(maskT[:, :], bank[5][:, 0:P], ACT.Copy).then_inc(w_ev, 1)
            nc.scalar.activation(wT[:, 0:3 * P], bank[6][:, 0:3 * P], ACT.Copy).then_inc(w_ev, 1)
            nc.scalar.activation(wT[:, 3 * P:7 * P], bank[4][:, :], ACT.Copy).then_inc(w_ev, 1)
            nc.scalar.activation(wT[:, 7 * P:8 * P], bank[5][:, P:2 * P], ACT.Copy).then_inc(w_ev, 1)
            nc.scalar.activation(smallT[:, :], bank[5][:, 2 * P:2 * P + SMALL], ACT.Copy).then_inc(w_ev, 1)
            nc.scalar.activation(wh_hi[:, :], bank[7][:, 0:3 * P], ACT.Copy).then_inc(w_hi, 1)
            for l in range(L):
                act.wait_ge(w_prod, l + 1)
                nc.scalar.activation(wx_hi[:, l * GATE:(l + 1) * GATE], bank[l][:, 0:GATE], ACT.Copy)\
                  .then_inc(w_hi, 1)
            act.wait_ge(w_v, W_FMX)
            nc.scalar.activation(fw[:, :], fw[:, :], ACT.Exp, bias=fmx[:, 0:1], accum_out=fsum[:, 0:1])\
              .then_inc(w_exp, 1)

            def step_a(k, m, has):
                if has(0):
                    act.wait_ge(a_tadj, k + 1)
                    if has(4):
                        act.wait_ge(a_y1, k - 3)
                    nc.scalar.activation(ADJT[m][:, :], bank[0][:, :], ACT.Copy).then_inc(a_adjT, 1)
                if has(0):
                    act.wait_ge(a_y0, k + 1)
                    nc.scalar.activation(YT0[:, :], bank[1][:, :], ACT.Copy).then_inc(a_yT0, 1)
                if has(2):
                    act.wait_ge(a_y1, k - 1)
                    nc.scalar.activation(YT1[:, :], bank[3][:, :], ACT.Copy).then_inc(a_yT1, 1)
                if has(4):
                    wait_apart(act, a_nm1, k - 3)
                    for i in range(G4):
                        last = nc.scalar.activation(x2[:, bass.ds(((k - 4) * G4 + i) * D, D)],
                                                    cols(WS1[m % 2], i), ACT.Identity,
                                                    bias=NM1[m % 2][:, i:i + 1], scale=RS1[m % 2][:, i:i + 1])
                    last.then_inc(a_x2, 1)
            run_a(act, step_a)

            def split_x(s, it):
                act.wait_ge(b_ldx[s], 16 * it + 16)
                nc.scalar.activation(HN_HI[s][:, :], X2S[s][:, :], ACT.Copy).then_inc(b_hnh[s], 1)

            def half_b(first, second, tails, after):
                if first and not second:
                    split_x(first[0], first[2])
                if second:
                    s, l, it = second
                    n1 = it * L + l + 1
                    act.wait_ge(b_R[s], n1)
                    nc.scalar.activation(RT[s][:, :], bank[4 * s + 0][:, :], ACT.Sigmoid,
                                         bias=brz[:, 0:1]).then_inc(b_r[s], 1)
                if first:
                    s, l, it = first
                    n1 = it * L + l + 1
                    if l == 0:
                        act.wait_ge(b_t0[s], it + 1)
                        nc.scalar.activation(HT_HI[s][:, :], bank[4 * s + 2][:, :], ACT.Copy)\
                          .then_inc(b_hth[s], 1)
                    else:
                        act.wait_ge(b_h[s], n1 - 1)
                        nc.scalar.activation(HT_HI[s][:, :], HT[s][:, :], ACT.Copy).then_inc(b_hth[s], 1)
                if tails[0]:
                    s, l, it = tails[0]
                    act.wait_ge(b_tp[s], it * L + L)
                    nc.scalar.activation(YB[s][:, :], bank[4 * s + 3][:, :], ACT.Copy).then_inc(b_ye[s], 1)
                if first:
                    s, l, it = first
                    n1 = it * L + l + 1
                    if l > 0:
                        act.wait_ge(b_tp[s], n1 - 1)
                        nc.scalar.activation(HN_HI[s][:, :], bank[4 * s + 3][:, :], ACT.Copy)\
                          .then_inc(b_hnh[s], 1)
                if second:
                    s, l, it = second
                    n1 = it * L + l + 1
                    act.wait_ge(b_Z[s], n1)
                    nc.scalar.activation(ZW[s][:, :], bank[4 * s + 1][:, :], ACT.Sigmoid,
                                         bias=brz[:, 1:2]).then_inc(b_z[s], 1)
                    nc.scalar.activation(WB[s][:, :], bank[4 * s + 1][:, :], ACT.Sigmoid,
                                         bias=nbz[:, 0:1], scale=-1.0).then_inc(b_w[s], 1)
                    act.wait_ge(b_t2[s], n1)
                    nc.scalar.activation(RT[s][:, :], RT[s][:, :], ACT.Tanh, bias=bih[:, 2:3])\
                      .then_inc(b_n[s], 1)
                if first:
                    s, l, it = first
                    n1 = it * L + l + 1
                    act.wait_ge(b_at[s], n1)
                    nc.scalar.activation(PT_HI[s][:, :], bank[4 * s + 3][:, :], ACT.Copy)\
                      .then_inc(b_ph[s], 1)
                if after:
                    split_x(after[0], after[2])
            act.wait_ge(w_v, W_BRZ)
            act.wait_ge(a_x2, STEPS_A)
            run_b(act, half_b)

            def apply_c(k, m, some):
                h = (m + 1) % 2
                for i in some:
                    c = h * GC + i
                    last = nc.scalar.activation(YO[:, c * D:(c + 1) * D],
                                                x2[:, bass.ds(((k - 3) * GC + i) * D, D)],
                                                ACT.Identity, bias=NMC[:, c:c + 1], scale=RSC[:, c:c + 1])
                last.then_inc(c_yoh, 1)

            def step_c(k, m, has):
                if has(1):
                    act.wait_ge(c_n, k)
                    nc.scalar.activation(TN[0:2 * SLOTS, :], psum[0:2 * SLOTS, 6 * 512:8 * 512], ACT.Copy)\
                      .then_inc(c_tn, 1)
                if has(0):
                    act.wait_ge(c_s, k + 1)
                    nc.scalar.activation(SP_T[:, :].rearrange("p (b x) -> p b x", b=2),
                                         psum[:, 0:2 * 512].rearrange("p (b x) -> p b x", b=2)[:, :, 0:CS // 2],
                                         ACT.Copy).then_inc(c_st, 1)
                if has(1):
                    act.wait_ge(c_o, k)
                    for g in range(NG):
                        nc.scalar.activation(slots(OT[:, :], g).rearrange("p (b s) c -> p b s c", b=2),
                                             slots2(6, g), ACT.Relu,
                                             bias=nwb2[:, g:g + 1], scale=nw[:, g:g + 1]).then_inc(c_ro, 1)
                if has(3):
                    wait_apart(act, c_nm, k - 2)
                    if has(5):
                        wait_apart(act, c_out[(m + 1) % 2], (k - 3 - (m + 1) % 2) * 8)
                    apply_c(k, m, range(ON_ACT // 2))
                if has(0):
                    act.wait_ge(c_h[0], k + 1)
                    for g in range(NG):
                        nc.scalar.activation(grp(HID[0], g), by_group(2, g), ACT.Relu,
                                             bias=b1T[:, g * HC:g * HC + 1]).then_inc(c_rh[0], 1)
                    act.wait_ge(c_t, k + 1)
                    nc.scalar.activation(slots(TT[:, :], 0), per_graph(by_group(0, 0), 0), ACT.Copy)\
                      .then_inc(c_tt, 1)
                if has(3):
                    apply_c(k, m, range(ON_ACT // 2, ON_ACT))
            for s in range(2):
                act.wait_ge(b_x3[s], ITERS * G4)
            run_c(act, step_c)

        @block.vector
        def _(dve):
            def norm(tile, st, mv, n, s_in, at, s_bs, s_mv):
                wait_apart(dve, s_in, at)
                for i in range(n):
                    last = nc.vector.bn_stats(st[:, 6 * i:6 * i + 6], tile[:, i * D:(i + 1) * D])
                last.then_inc(s_bs, 1)
                wait_apart(dve, s_bs, at)
                for i in range(n):
                    last = nc.vector.bn_aggr(mv[:, 2 * i:2 * i + 2], st[:, 6 * i:6 * i + 6])
                last.then_inc(s_mv, 1)

            def apply(dst, tile, mv, rs, n, s_rs, at, s_out):
                dve.wait_ge(s_rs, at)
                for i in range(n):
                    last = nc.vector.tensor_scalar(dst(i), tile[:, i * D:(i + 1) * D], mv[:, 2 * i:2 * i + 1],
                                                   rs[:, i:i + 1], ALU.subtract, ALU.mult)
                last.then_inc(s_out, 1)

            dve.wait_ge(w_hi, 1)
            nc.vector.tensor_tensor(wh_lo[:, :], bank[7][:, 0:3 * P], wh_hi[:, :].bitcast(F32),
                                    ALU.subtract).then_inc(w_lo, 1)
            for l in range(L):
                dve.wait_ge(w_hi, l + 2)
                sl = slice(l * GATE, (l + 1) * GATE)
                nc.vector.tensor_tensor(wx_lo[:, sl], bank[l][:, 0:GATE], wx_hi[:, sl].bitcast(F32),
                                        ALU.subtract).then_inc(w_lo, 1)

            count = [0]

            def link(ins):
                count[0] += 1
                ins.then_inc(w_v, 1)
                dve.wait_ge(w_v, count[0])

            dve.wait_ge(w_ld_fw, 16)
            dve.wait_ge(w_ev, 5)
            link(nc.vector.tensor_tensor(brz[:, :], bih[:, 0:2], bhh[:, 0:2], ALU.add))
            link(nc.vector.tensor_scalar(nbz[:, :], brz[:, 1:2], -1.0, None, ALU.mult))
            link(nc.vector.tensor_reduce(fmx[:, :], fw[:, :], AX_X, ALU.max))
            link(nc.vector.tensor_scalar(fmx[:, :], fmx[:, :], -1.0, None, ALU.mult))
            dve.wait_ge(w_ld_a25, 16)
            link(nc.vector.tensor_scalar(adj25[:, 0:NODES * NODES:NODES + 1],
                                         adj25[:, 0:NODES * NODES:NODES + 1], 1.0, None, ALU.add))
            a25 = adj25[:, :].rearrange("s (i j) -> s i j", i=NODES)
            ca = [cmp_a[:, SQ_OFFS[g]:SQ_OFFS[g] + SQ[g]].rearrange("s (i j) -> s i j", i=SIZES[g])
                  for g in range(NG)]
            for g in range(NG):
                r0 = 0
                for i0, ni in RUNS[g]:
                    c0 = 0
                    for j0, nj in RUNS[g]:
                        last = nc.vector.tensor_copy(ca[g][:, r0:r0 + ni, c0:c0 + nj],
                                                     a25[:, i0:i0 + ni, j0:j0 + nj])
                        c0 += nj
                    r0 += ni
            link(last)
            for g in range(NG):
                last = nc.vector.tensor_reduce(deg[:, OFFS[g]:OFFS[g] + SIZES[g]], ca[g], AX_X, ALU.add)
            link(last)
            link(nc.vector.tensor_scalar(deg0[:, :], deg[:, :], 0.0, None, ALU.is_equal))
            link(nc.vector.tensor_tensor(deg[:, :], deg[:, :], deg0[:, :], ALU.add))
            link(nc.vector.tensor_scalar(deg0[:, :], deg0[:, :], -1.0, 1.0, ALU.mult, ALU.add))
            dve.wait_ge(w_pow, 1)
            link(nc.vector.tensor_tensor(dinv[:, :], dinv[:, :], deg0[:, :], ALU.mult))
            an = [anT[:, SQ_OFFS[g]:SQ_OFFS[g] + SQ[g]].rearrange("s (j i) -> s j i", i=SIZES[g])
                  for g in range(NG)]
            for g in range(NG):
                d = dinv[:, OFFS[g]:OFFS[g] + SIZES[g]]
                last = nc.vector.tensor_tensor(an[g], ca[g].rearrange("s i j -> s j i"),
                                               d.unsqueeze(1).to_broadcast([P, SIZES[g], SIZES[g]]), ALU.mult)
            link(last)
            for g in range(NG):
                d = dinv[:, OFFS[g]:OFFS[g] + SIZES[g]]
                last = nc.vector.tensor_tensor(an[g], an[g],
                                               d.unsqueeze(2).to_broadcast([P, SIZES[g], SIZES[g]]), ALU.mult)
            link(last)
            dve.wait_ge(w_exp, 1)
            link(nc.vector.reciprocal(fsum[:, :], fsum[:, :]))
            link(nc.vector.tensor_scalar(nw[:, :], fw[:, :], fsum[:, 0:1], None, ALU.mult))
            link(nc.vector.tensor_tensor(nwb2[:, :], nw[:, :], b2T[:, :], ALU.mult))
            assert count[0] == W_ALL
            dve.wait_ge(w_ld_misc, 16 * 7)

            def step_a(k, m, has):
                if has(4):
                    dve.wait_ge(a_rs1, k - 3)
                    nc.vector.scalar_tensor_tensor(NM1[m % 2][:, :], MV1[m % 2][:, 0:2 * G4:2], -1.0,
                                                   RS1[m % 2][:, :], ALU.mult, ALU.mult).then_inc(a_nm1, 1)
                if has(1):
                    dve.wait_ge(a_z0, k)
                    nc.vector.tensor_tensor(v4(U[:, :]), v4(bank[2][:, :]), bc4(bias0_bc), ALU.add)\
                      .then_inc(a_u, 1)
                    dve.wait_ge(a_u, k)
                    if has(2):
                        dve.wait_ge(a_w0, k - 1)
                    nc.vector.tensor_scalar(V[:, :], U[:, :], 0.0, alpha[:, 0:1], ALU.min, ALU.mult)\
                      .then_inc(a_m, 1)
                    dve.wait_ge(a_m, k)
                    nc.vector.scalar_tensor_tensor(V[:, :], U[:, :], 0.0, V[:, :], ALU.max, ALU.add)\
                      .then_inc(a_v, 1)
                if has(2):
                    p = m % 2
                    apply(lambda i: cols(X1[(m - 2) % 4], i), WS0[p], MV0[p], RS0[p], G4, a_rs0, k - 1, a_x1)
                if has(3):
                    p = (m - 3) % 2
                    dve.wait_ge(a_z1, k - 2)
                    dve.wait_ge(a_x1b, k - 2)
                    if has(5):
                        dve.wait_ge(a_x2, k - 4)
                    nc.vector.tensor_tensor(WS1[p][:, :], bank[4][:, :], X1B[p][:, :], ALU.add)\
                      .then_inc(a_w1, 1)
                    norm(WS1[p], ST1, MV1[p], G4, a_w1, k - 2, a_bs1, a_mv1)
                if has(1):
                    p = (m - 1) % 2
                    norm(WS0[p], ST0, MV0[p], G4, a_w0, k, a_bs0, a_mv0)
            run_a(dve, step_a)

            def apply_some(tail, first_graph):
                s, l, it = tail
                wait_apart(dve, b_rs[s], it + 1)
                for i in range(first_graph, first_graph + G4 // 2):
                    nc.vector.tensor_scalar(x2[:, bass.ds(((it * 2 + s) * G4 + i) * D, D)], cols(YB[s], i),
                                            MVB[s][:, 2 * i:2 * i + 1], RSB[s][:, i:i + 1],
                                            ALU.subtract, ALU.mult).then_inc(b_x3[s], 1)

            def split_x(s, it):
                dve.wait_ge(b_lda[s], 16 * it + 16)
                nc.vector.tensor_scalar(A16[s][:, :], ADJR[s][:, :], 0.0, None, ALU.not_equal)\
                  .then_inc(b_a16[s], 1)
                dve.wait_ge(b_hnh[s], it * L + 1)
                nc.vector.tensor_tensor(HN_LO[s][:, :], X2S[s][:, :], HN_HI[s][:, :], ALU.subtract)\
                  .then_inc(b_hnl[s], 1)

            def half_b(first, second, tails, after):
                if first and not second:
                    split_x(first[0], first[2])
                if second:
                    s, l, it = second
                    n1 = it * L + l + 1
                    dve.wait_ge(b_r[s], n1)
                    nc.vector.scalar_tensor_tensor(RT[s][:, :], bank[4 * s + 2][:, :], bhh[:, 2:3],
                                                   RT[s][:, :], ALU.add, ALU.mult).then_inc(b_t1[s], 1)
                if first and first[1] == 0:
                    s, l, it = first
                    dve.wait_ge(b_hth[s], it * L + 1)
                    if not (isinstance(it, int) and it == 0):
                        dve.wait_ge(b_tp[s], it * L)
                    nc.vector.tensor_copy(HT[s][:, :], bank[4 * s + 2][:, :]).then_inc(b_h0[s], 1)
                if second:
                    s, l, it = second
                    n1 = it * L + l + 1
                    dve.wait_ge(b_t1[s], n1)
                    dve.wait_ge(b_I[s], n1)
                    nc.vector.tensor_tensor(RT[s][:, :], bank[4 * s + 3][:, :], RT[s][:, :], ALU.add)\
                      .then_inc(b_t2[s], 1)
                if first:
                    s, l, it = first
                    n1 = it * L + l + 1
                    if l > 0:
                        dve.wait_ge(b_hnh[s], n1)
                        nc.vector.tensor_tensor(HN_LO[s][:, :], bank[4 * s + 3][:, :], HN_HI[s][:, :],
                                                ALU.subtract).then_inc(b_hnl[s], 1)
                if tails[1]:
                    s, l, it = tails[1]
                    wait_apart(dve, b_y[s], it + 1)
                    for i in range(G4):
                        last = nc.vector.bn_stats(STB[s][:, 6 * i:6 * i + 6], cols(YB[s], i))
                    last.then_inc(b_bs[s], 1)
                if tails[2]:
                    apply_some(tails[2], 0)
                if second:
                    s, l, it = second
                    n1 = it * L + l + 1
                    dve.wait_ge(b_n[s], n1)
                    dve.wait_ge(b_w[s], n1)
                    nc.vector.tensor_tensor(RT[s][:, :], RT[s][:, :], WB[s][:, :], ALU.mult)\
                      .then_inc(b_q[s], 1)
                if first:
                    s, l, it = first
                    n1 = it * L + l + 1
                    dve.wait_ge(b_ph[s], n1)
                    nc.vector.tensor_tensor(PT_LO[s][:, :], bank[4 * s + 3][:, :],
                                            PT_HI[s][:, :].bitcast(F32), ALU.subtract).then_inc(b_pl[s], 1)
                if second:
                    s, l, it = second
                    n1 = it * L + l + 1
                    dve.wait_ge(b_q[s], n1)
                    dve.wait_ge(b_zh[s], n1)
                    nc.vector.tensor_tensor(HT[s][:, :], RT[s][:, :], ZH[s][:, :], ALU.add)\
                      .then_inc(b_h[s], 1)
                if after:
                    split_x(after[0], after[2])
                if tails[1]:
                    s, l, it = tails[1]
                    wait_apart(dve, b_bs[s], it + 1)
                    for i in range(G4):
                        last = nc.vector.bn_aggr(MVB[s][:, 2 * i:2 * i + 2], STB[s][:, 6 * i:6 * i + 6])
                    last.then_inc(b_mv[s], 1)
                if tails[2]:
                    apply_some(tails[2], G4 // 2)
            run_b(dve, half_b)

            def step_c(k, m, has):
                if has(2):
                    dve.wait_ge(c_f, k - 1)
                    if has(4):
                        dve.wait_ge(c_yop, k - 3)
                    for h in range(2):
                        w = GC // 2 * D
                        xs = x2[0:NODES, bass.ds(((k - 2) * 2 + h) * w, w)]
                        nc.vector.tensor_tensor(xs, psum[0:NODES, 2 * 512 + h * w:2 * 512 + (h + 1) * w], xs, ALU.add)\
                          .then_inc(c_x, 1)
                    wait_apart(dve, c_x, 2 * (k - 1))
                    for i in range(GC):
                        last = nc.vector.bn_stats(STC[:, 6 * i:6 * i + 6],
                                                  x2[:, bass.ds(((k - 2) * GC + i) * D, D)])
                    last.then_inc(c_bs, 1)
                    wait_apart(dve, c_bs, k - 1)
                    for i in range(GC):
                        last = nc.vector.bn_aggr(MVC[:, (m * GC + i) * 2:(m * GC + i) * 2 + 2],
                                                 STC[:, 6 * i:6 * i + 6])
                    last.then_inc(c_mv, 1)
                if has(1):
                    ov = OT[:, :].rearrange("p (s c) -> p s c", c=SLOTS)
                    dve.wait_ge(c_ro, NG * k)
                    done = 0
                    for g in range(1, NG):
                        at = OFFS[g]
                        for n0, cnt in RUNS[g]:
                            if done:
                                dve.wait_ge(c_add, (k - 1) * ADDS + done)
                            nc.vector.tensor_tensor(ov[:, :, n0:n0 + cnt], ov[:, :, n0:n0 + cnt],
                                                    ov[:, :, at:at + cnt], ALU.add).then_inc(c_add, 1)
                            at += cnt
                            done += 1
                if has(0):
                    dve.wait_ge(c_h[1], k + 1)
                    for g in range(NG):
                        nc.vector.tensor_scalar(grp(HID[1], g), by_group(4, g),
                                                b1T[:, g * HC + 1:g * HC + 2], 0.0, ALU.add, ALU.max)\
                          .then_inc(c_rh[1], 1)
                    dve.wait_ge(c_t, k + 1)
                    for g in range(1, NG):
                        last = nc.vector.tensor_copy(slots(TT[:, :], g), per_graph(by_group(0, g), g))
                    last.then_inc(c_tts, 1)
                if has(2):
                    dve.wait_ge(c_rs, k - 1)
                    nc.vector.scalar_tensor_tensor(NMC[:, m * GC:(m + 1) * GC],
                                                   MVC[:, m * GC * 2:(m + 1) * GC * 2:2], -1.0,
                                                   RSC[:, m * GC:(m + 1) * GC], ALU.mult, ALU.mult)\
                      .then_inc(c_nm, 1)
            run_c(dve, step_c)

        @block.tensor
        def _(pe):
            mm = nc.tensor.matmul

            pe.wait_ge(w_ident, 2)
            pe.wait_ge(w_ld_tr, 16 * 8)
            nc.tensor.transpose(bank[5][:, 0:P], mask_sb[:, :], ident[:, :])
            nc.tensor.transpose(bank[5][:, 2 * P:2 * P + SMALL], small[:, :], ident[0:SMALL, 0:SMALL])
            for g in range(3):
                nc.tensor.transpose(bank[6][:, g * P:(g + 1) * P], cols(sc_raw, g), ident[:, :])
                nc.tensor.transpose(bank[7][:, g * P:(g + 1) * P], cols(sc_raw, 3 + g), ident[:, :])
            for l in range(L):
                dst = bank[4][:, l * P:(l + 1) * P] if l < 4 else bank[5][:, P:2 * P]
                last = nc.tensor.transpose(dst, cols(sc_raw, 6 + l), ident[:, :])
            last.then_inc(w_tr, 1)
            pe.wait_ge(w_ev, 5)
            for l in range(L):
                mm(bank[l][:, 0:GATE], cols(wT, 3 + l), wT[:, 0:GATE], start=True, stop=True)\
                    .then_inc(w_prod, 1)
            pe.wait_ge(w_lo, L + 1)
            pe.wait_ge(w_ld_misc, 16 * 7)

            def four(dst, lhs, rhs, signal):
                for i in range(G4):
                    last = mm(cols(dst, i), lhs(i), rhs(i), start=True, stop=True)
                last.then_inc(signal, 1)

            def step_a(k, m, has):
                if has(0):
                    pe.wait_ge(a_ld[m], (k - m) * 8 + 32)
                    if has(1):
                        pe.wait_ge(a_adjT, k)
                    for i in range(G4):
                        last = nc.tensor.transpose(cols(bank[0], i), cols(ADJ[m], i), ident[:, :])
                    last.then_inc(a_tadj, 1)
                if has(3):
                    pe.wait_ge(a_yT1, k - 2)
                    if has(4):
                        pe.wait_ge(a_w1, k - 3)
                    four(bank[4], lambda i: cols(YT1, i), lambda i: w1_sb[:, :], a_z1)
                if has(0):
                    pe.wait_ge(a_adjT, k + 1)
                    four(bank[1], lambda i: cols(X0[m], i), lambda i: cols(ADJT[m], i), a_y0)
                if has(0):
                    pe.wait_ge(a_yT0, k + 1)
                    if has(1):
                        pe.wait_ge(a_u, k)
                    four(bank[2], lambda i: cols(YT0, i), lambda i: w0_sb[:, :], a_z0)
                if has(2):
                    pe.wait_ge(a_x1, k - 1)
                    mp = (m - 2) % 4
                    four(bank[3], lambda i: cols(X1[mp], i), lambda i: cols(ADJT[mp], i), a_y1)
            run_a(pe, step_a)

            def hi_passes(dst, w_h, w_l, col, h, start):
                mm(dst[:, :], w_h[:, col:col + P], h[:, :], start=start, stop=False)
                mm(dst[:, :], w_l[:, col:col + P], h[:, :], start=False, stop=False)

            def lo_pass(dst, w_h, col, lo, stop):
                return mm(dst[:, :], w_h[:, col:col + P], lo[:, :], start=False, stop=stop)

            def start(s, it):
                pe.wait_ge(b_ldx[s], 16 * it + 16)
                if not (isinstance(it, int) and it == 0):
                    pe.wait_ge(b_t1[s], it * L)
                for i in range(G4):
                    last = nc.tensor.transpose(cols(bank[4 * s + 2], i), cols(X2S[s], i), ident[:, :])
                last.then_inc(b_t0[s], 1)

            def half_b(first, second, tails, after):
                if first and not second:
                    start(first[0], first[2])
                if second:
                    s, l, it = second
                    g = l * GATE
                    hi_passes(bank[4 * s + 3], wx_hi, wx_lo, g + 2 * P, PT_HI[s], True)
                    lo_pass(bank[4 * s + 3], wx_hi, g + 2 * P, PT_LO[s], True).then_inc(b_I[s], 1)
                    lo_pass(bank[4 * s + 1], wx_hi, g + P, PT_LO[s], True).then_inc(b_Z[s], 1)
                if first:
                    s, l, it = first
                    n1 = it * L + l + 1
                    pe.wait_ge(b_hth[s], n1)
                    for b in range(3):
                        if l == 0 and b == 2:
                            pe.wait_ge(b_h0[s], it + 1)
                        hi_passes(bank[4 * s + b], wh_hi, wh_lo, b * P, HT_HI[s], True)
                    if l == 0:
                        pe.wait_ge(b_a16[s], it + 1)
                    pe.wait_ge(b_hnl[s], n1)
                    if l == 0 and not (isinstance(it, int) and it == 0):
                        pe.wait_ge(b_ye[s], it)
                    for i in range(G4):
                        mm(cols(bank[4 * s + 3], i), cols(HN_HI[s], i), cols(A16[s], i), start=True, stop=False)
                        last = mm(cols(bank[4 * s + 3], i), cols(HN_LO[s], i), cols(A16[s], i),
                                  start=False, stop=True)
                    last.then_inc(b_at[s], 1)
                    pe.wait_ge(b_htl[s], n1)
                    for b in range(3):
                        lo_pass(bank[4 * s + b], wh_hi, b * P, HT_LO[s], b == 2)
                    pe.wait_ge(b_ph[s], n1)
                    for b in range(2):
                        hi_passes(bank[4 * s + b], wx_hi, wx_lo, l * GATE + b * P, PT_HI[s], False)
                    pe.wait_ge(b_pl[s], n1)
                    lo_pass(bank[4 * s + 0], wx_hi, l * GATE, PT_LO[s], True).then_inc(b_R[s], 1)
                if after:
                    start(after[0], after[2])
                if second:
                    s, l, it = second
                    n1 = it * L + l + 1
                    pe.wait_ge(b_h[s], n1)
                    for i in range(G4):
                        last = nc.tensor.transpose(cols(bank[4 * s + 3], i), cols(HT[s], i), ident[:, :])
                    last.then_inc(b_tp[s], 1)
            pe.wait_ge(a_x2, STEPS_A)
            run_b(pe, half_b)

            W2 = 2 * SLOTS

            def step_c(k, m, has):
                if has(2):
                    pe.wait_ge(c_add, (k - 1) * ADDS)
                    for i in range(GC):
                        last = nc.tensor.transpose(psum[0:NODES, 2 * 512 + i * P:2 * 512 + (i + 1) * P],
                                                   OT[:, i * SLOTS:i * SLOTS + NODES], ident[:, :])
                    last.then_inc(c_f, 1)
                if has(1):
                    pe.wait_ge(c_tt, k)
                    pe.wait_ge(c_tts, k)
                    for i in range(PAIRS):
                        last = nc.tensor.transpose(psum[0:W2, 6 * 512 + i * P:6 * 512 + (i + 1) * P],
                                                   TT[:, i * W2:(i + 1) * W2], ident[:, :])
                    last.then_inc(c_n, 1)
                if has(0):
                    pe.wait_ge(c_ldx, 32 * k + 32)
                    for i in range(PAIRS):
                        c = i % (PAIRS // 2) * W2
                        last = mm(bank[i // (PAIRS // 2)][:, c:c + W2], X3S[0:2 * NODES, i * D:(i + 1) * D],
                                  m2[0:2 * NODES, bass.ds((k * PAIRS + i) * W2, W2)], start=True, stop=True)
                    last.then_inc(c_s, 1)
                if has(1):
                    pe.wait_ge(c_tn, k)
                    for i in range(PAIRS):
                        c = i % (PAIRS // 2) * W2
                        last = mm(bank[6 + i // (PAIRS // 2)][:, c:c + W2], TN[0:W2, i * P:(i + 1) * P],
                                  n2[0:W2, bass.ds(((k - 1) * PAIRS + i) * W2, W2)], start=True, stop=True)
                    last.then_inc(c_o, 1)
                if has(0):
                    pe.wait_ge(c_st, k + 1)
                    if has(2):
                        pe.wait_ge(c_x, 2 * (k - 1))
                    for c in range(HC):
                        for g in range(NG):
                            last = mm(by_group(2 + 2 * c, g), v1[:, (g * HC + c) * P:(g * HC + c + 1) * P],
                                      slots(SP_T[:, :], g), start=True, stop=True)
                        last.then_inc(c_h[c], 1)
                    for g in range(NG):
                        for c in range(HC):
                            pe.wait_ge(c_rh[c], NG * k + g + 1)
                            last = mm(by_group(0, g), v2[:, (g * HC + c) * P:(g * HC + c + 1) * P],
                                      grp(HID[c], g), start=c == 0, stop=c == HC - 1)
                    last.then_inc(c_t, 1)
            pe.wait_ge(l3_ld, 16 * L3_LOADS)
            for s in range(2):
                pe.wait_ge(b_x3[s], ITERS * G4)
            run_c(pe, step_c)


W_BRZ, W_FMX, W_DEG, W_AN, W_ALL = 2, 4, 9, 13, 16
ADDS = sum(len(r) for r in RUNS[1:])
L3_LOADS = 2 * sum(len(r) for r in RUNS) + 2 * NG


_INS = ['x', 'adj', 'nodemask', 'L0_gnn_W', 'L0_gnn_bias', 'L0_gnn_prelu_a', 'L1_gnn_weight', 'L1_gnn_bias',
        'L2_gnn_weight', 'L2_gnn_w_ih', 'L2_gnn_w_hh', 'L2_gnn_b_ih', 'L2_gnn_b_hh', 'L3_gnn_W1', 'L3_gnn_b1',
        'L3_gnn_W2', 'L3_gnn_b2', 'L3_gnn_fusion_w']


def kernel(**inputs):
    import numpy as _np
    import concourse.bacc as _bacc
    from concourse import mybir as _mybir
    from concourse.bass_utils import run_bass_kernel_spmd as _run

    nc = _bacc.Bacc("TRN2", target_bir_lowering=False, num_devices=1)
    arrays, args = {}, []
    for name in _INS:
        a = _np.ascontiguousarray(inputs[name])
        if a.ndim == 0:
            a = a.reshape(1)
        arrays[f"in_{name}_dram"] = a
        args.append(nc.dram_tensor(f"in_{name}_dram", a.shape, _mybir.dt.from_np(a.dtype), kind="ExternalInput").ap())
    shape = tuple(inputs['x'].shape)
    args.append(nc.dram_tensor("out_0_dram", shape, _mybir.dt.float32, kind="ExternalOutput").ap())
    graph_stack_kernel(nc, *args)
    r = _run(nc, [arrays], core_ids=[0])
    return r.results[0]["out_0_dram"]
```
